# Optimizing a Trainium2 kernel written in Bass

```python
import numpy as np
import jax
import jax.numpy as jnp

def _softmax(x, axis=-1):
    return jax.nn.softmax(x, axis=axis)

def _gelu(x):
    return jax.nn.gelu(x, approximate=True)

def _silu(x):
    return jax.nn.silu(x)

def _sigmoid(x):
    return jax.nn.sigmoid(x)

def _layernorm(x, axis=-1, eps=1e-05):
    m = jnp.mean(x, axis=axis, keepdims=True)
    v = jnp.var(x, axis=axis, keepdims=True)
    return (x - m) / jnp.sqrt(v + eps)

def _scatter_add(tgt, idx, src, axis=0):
    return tgt.at[idx].add(src)

def _segment_sum(src, seg, n):
    return jax.ops.segment_sum(src, seg, n)
kernel_name = 'mk_seq_postln_d2_jaxref_r8_027044'

def setup_inputs(seed: int=0):
    np.random.seed(seed)
    _w = jnp.asarray

    def _L0_attn_setup():
        import jax, jax.numpy as jnp
        import numpy as np
        FEATURE_DIM = 16
        NUM_HEADS = 16
        HEAD_DIM = 64
        R2 = float(np.sqrt(2.0))
        RD = float(np.sqrt(FEATURE_DIM))
        RRD = float(np.sqrt(RD))
        RMS_EPS = 1e-05

        def taylor_exp(x):
            x2 = (x[..., :, None] * x[..., None, :]).reshape(*x.shape[:-1], FEATURE_DIM * FEATURE_DIM) / R2
            ones = jnp.ones_like(x[..., :1])
            return jnp.concatenate([ones, x / RRD, x2 / RD], axis=-1)

        def _reference_tuple_inner(hidden_states, Wq, Wk, Wv, Wo, g_weight):
            b, l, _ = hidden_states.shape
            q = (hidden_states @ Wq.T).reshape(b, l, NUM_HEADS, FEATURE_DIM).transpose(0, 2, 1, 3)
            k = (hidden_states @ Wk.T).reshape(b, l, NUM_HEADS, FEATURE_DIM).transpose(0, 2, 1, 3)
            v = (hidden_states @ Wv.T).reshape(b, l, NUM_HEADS, HEAD_DIM).transpose(0, 2, 1, 3)
            qf = taylor_exp(q)
            kf = taylor_exp(k)
            A_qk = jnp.einsum('bhnd,bhmd->bhnm', qf, kf)
            A_qk = jnp.tril(A_qk)
            y = jnp.einsum('bhnm,bhme->bhne', A_qk, v)
            kv_state = jnp.einsum('bhnd,bhnf->bhfd', kf, v)[:, :, None]
            rms = jax.lax.rsqrt(jnp.mean(y * y, axis=-1, keepdims=True) + RMS_EPS)
            y = y * rms * g_weight
            y = y.transpose(0, 2, 1, 3).reshape(b, l, NUM_HEADS * HEAD_DIM)
            out = y @ Wo.T
            return (out, kv_state)
        key = jax.random.key(seed)
        ks = jax.random.split(key, 5)
        b, l, d_model = (4, 256, 128)
        inp = {'hidden_states': jax.random.normal(ks[0], (b, l, d_model), dtype=jnp.float32), 'Wq': jax.random.normal(ks[1], (FEATURE_DIM * NUM_HEADS, d_model), dtype=jnp.float32) * 0.02, 'Wk': jax.random.normal(ks[2], (FEATURE_DIM * NUM_HEADS, d_model), dtype=jnp.float32) * 0.02, 'Wv': jax.random.normal(ks[3], (NUM_HEADS * HEAD_DIM, d_model), dtype=jnp.float32) * 0.02, 'Wo': jax.random.normal(ks[4], (d_model, NUM_HEADS * HEAD_DIM), dtype=jnp.float32) * 0.02, 'g_weight': jnp.ones((HEAD_DIM,), dtype=jnp.float32)}
        return inp
    _L0_attn_in = _L0_attn_setup()

    def _L0_ffn_setup():
        import jax, jax.numpy as jnp
        import numpy as np
        D_MODEL = 128
        HIDDEN = 512
        N_ROUTING = 2
        key = jax.random.key(seed)
        ks = jax.random.split(key, 10)
        s = 0.02
        x = jax.random.normal(ks[0], (4, 512, D_MODEL), dtype=jnp.float32)
        gate_w = jax.random.normal(ks[1], (N_ROUTING, D_MODEL), dtype=jnp.float32) * s
        w1 = jax.random.normal(ks[2], (N_ROUTING, D_MODEL, HIDDEN), dtype=jnp.float32) * s
        b1 = jax.random.normal(ks[3], (N_ROUTING, HIDDEN), dtype=jnp.float32) * s
        w2 = jax.random.normal(ks[4], (N_ROUTING, HIDDEN, D_MODEL), dtype=jnp.float32) * s
        b2 = jax.random.normal(ks[5], (N_ROUTING, D_MODEL), dtype=jnp.float32) * s
        sw1 = jax.random.normal(ks[6], (D_MODEL, HIDDEN), dtype=jnp.float32) * s
        sb1 = jax.random.normal(ks[7], (HIDDEN,), dtype=jnp.float32) * s
        sw2 = jax.random.normal(ks[8], (HIDDEN, D_MODEL), dtype=jnp.float32) * s
        sb2 = jax.random.normal(ks[9], (D_MODEL,), dtype=jnp.float32) * s
        return {'x': x, 'gate_w': gate_w, 'w1': w1, 'b1': b1, 'w2': w2, 'b2': b2, 'sw1': sw1, 'sb1': sb1, 'sw2': sw2, 'sb2': sb2}
    _L0_ffn_in = _L0_ffn_setup()

    def _L1_attn_setup():
        import math
        import jax, jax.numpy as jnp
        import numpy as np
        D = 128
        NH = 16
        DH = D // NH

        def _rope(q, k, base=10000.0):
            half = q.shape[-1] // 2
            freqs = jnp.arange(half, dtype=q.dtype) / half
            theta = 1.0 / base ** freqs
            t = jnp.arange(q.shape[-2], dtype=q.dtype)
            ang = t[:, None] * theta[None, :]
            cos = jnp.cos(ang)[None, None, :, :]
            sin = jnp.sin(ang)[None, None, :, :]

            def rot(x):
                x1, x2 = (x[..., :half], x[..., half:])
                return jnp.concatenate([x1 * cos - x2 * sin, x1 * sin + x2 * cos], axis=-1)
            return (rot(q), rot(k))
        key = jax.random.key(seed)
        k1, k2, k3 = jax.random.split(key, 3)
        x = jax.random.normal(k1, (2, 256, D), dtype=jnp.float32)
        s = 1.0 / math.sqrt(D)
        W_qkv = jax.random.normal(k2, (D, 3 * D), dtype=jnp.float32) * s
        W_o = jax.random.normal(k3, (D, D), dtype=jnp.float32) * s
        return {'x': x, 'W_qkv': W_qkv, 'W_o': W_o}
    _L1_attn_in = _L1_attn_setup()

    def _L1_ffn_setup():
        import jax, jax.numpy as jnp
        import numpy as np
        B, S, D, F, E, K = (2, 256, 128, 256, 8, 2)
        key = jax.random.key(seed)
        ks = jax.random.split(key, 5)
        scale = 0.02
        return {'x': jax.random.normal(ks[0], (B, S, D), dtype=jnp.float32), 'Wg': jax.random.normal(ks[1], (E, D), dtype=jnp.float32) * scale, 'W1': jax.random.normal(ks[2], (E, F, D), dtype=jnp.float32) * scale, 'W2': jax.random.normal(ks[3], (E, F, D), dtype=jnp.float32) * scale, 'W3': jax.random.normal(ks[4], (E, D, F), dtype=jnp.float32) * scale}
    _L1_ffn_in = _L1_ffn_setup()
    _d = {'L0_attn_hidden_states': _L0_attn_in['hidden_states'], 'L0_attn_Wq': _L0_attn_in['Wq'], 'L0_attn_Wk': _L0_attn_in['Wk'], 'L0_attn_Wv': _L0_attn_in['Wv'], 'L0_attn_Wo': _L0_attn_in['Wo'], 'L0_attn_g_weight': _L0_attn_in['g_weight'], 'L0_ffn_gate_w': _L0_ffn_in['gate_w'], 'L0_ffn_w1': _L0_ffn_in['w1'], 'L0_ffn_b1': _L0_ffn_in['b1'], 'L0_ffn_w2': _L0_ffn_in['w2'], 'L0_ffn_b2': _L0_ffn_in['b2'], 'L0_ffn_sw1': _L0_ffn_in['sw1'], 'L0_ffn_sb1': _L0_ffn_in['sb1'], 'L0_ffn_sw2': _L0_ffn_in['sw2'], 'L0_ffn_sb2': _L0_ffn_in['sb2'], 'L1_attn_W_qkv': _L1_attn_in['W_qkv'], 'L1_attn_W_o': _L1_attn_in['W_o'], 'L1_ffn_Wg': _L1_ffn_in['Wg'], 'L1_ffn_W1': _L1_ffn_in['W1'], 'L1_ffn_W2': _L1_ffn_in['W2'], 'L1_ffn_W3': _L1_ffn_in['W3']}
    _x0 = _d['L0_attn_hidden_states']
    _d['L0_attn_hidden_states'] = jax.random.normal(jax.random.fold_in(jax.random.key(seed), 1), (8, 256, 128), dtype=_x0.dtype)
    del _x0
    return _d

def reference(L0_attn_hidden_states, L0_attn_Wq, L0_attn_Wk, L0_attn_Wv, L0_attn_Wo, L0_attn_g_weight, L0_ffn_gate_w, L0_ffn_w1, L0_ffn_b1, L0_ffn_w2, L0_ffn_b2, L0_ffn_sw1, L0_ffn_sb1, L0_ffn_sw2, L0_ffn_sb2, L1_attn_W_qkv, L1_attn_W_o, L1_ffn_Wg, L1_ffn_W1, L1_ffn_W2, L1_ffn_W3):

    def _L0_attn_ref(hidden_states, Wq, Wk, Wv, Wo, g_weight):
        import jax, jax.numpy as jnp
        import numpy as np
        FEATURE_DIM = 16
        NUM_HEADS = 16
        HEAD_DIM = 64
        R2 = float(np.sqrt(2.0))
        RD = float(np.sqrt(FEATURE_DIM))
        RRD = float(np.sqrt(RD))
        RMS_EPS = 1e-05

        def taylor_exp(x):
            x2 = (x[..., :, None] * x[..., None, :]).reshape(*x.shape[:-1], FEATURE_DIM * FEATURE_DIM) / R2
            ones = jnp.ones_like(x[..., :1])
            return jnp.concatenate([ones, x / RRD, x2 / RD], axis=-1)

        def _reference_tuple_inner(hidden_states, Wq, Wk, Wv, Wo, g_weight):
            b, l, _ = hidden_states.shape
            q = (hidden_states @ Wq.T).reshape(b, l, NUM_HEADS, FEATURE_DIM).transpose(0, 2, 1, 3)
            k = (hidden_states @ Wk.T).reshape(b, l, NUM_HEADS, FEATURE_DIM).transpose(0, 2, 1, 3)
            v = (hidden_states @ Wv.T).reshape(b, l, NUM_HEADS, HEAD_DIM).transpose(0, 2, 1, 3)
            qf = taylor_exp(q)
            kf = taylor_exp(k)
            A_qk = jnp.einsum('bhnd,bhmd->bhnm', qf, kf)
            A_qk = jnp.tril(A_qk)
            y = jnp.einsum('bhnm,bhme->bhne', A_qk, v)
            kv_state = jnp.einsum('bhnd,bhnf->bhfd', kf, v)[:, :, None]
            rms = jax.lax.rsqrt(jnp.mean(y * y, axis=-1, keepdims=True) + RMS_EPS)
            y = y * rms * g_weight
            y = y.transpose(0, 2, 1, 3).reshape(b, l, NUM_HEADS * HEAD_DIM)
            out = y @ Wo.T
            return (out, kv_state)
        return _reference_tuple_inner(hidden_states, Wq, Wk, Wv, Wo, g_weight)[0]

    def _L0_ffn_ref(x, gate_w, w1, b1, w2, b2, sw1, sb1, sw2, sb2):
        import jax, jax.numpy as jnp
        import numpy as np
        D_MODEL = 128
        HIDDEN = 512
        N_ROUTING = 2
        B, S, D = x.shape
        xf = x.reshape(-1, D)
        gate_scores = xf @ gate_w.T
        gate_probs = jax.nn.softmax(gate_scores, axis=-1)
        top1 = jnp.argmax(gate_probs, axis=-1)
        one_hot = jax.nn.one_hot(top1, N_ROUTING, dtype=xf.dtype)
        masked = xf[None, :, :] * one_hot.T[:, :, None]
        h = jax.nn.relu(jnp.einsum('end,edh->enh', masked, w1) + b1[:, None, :])
        expert_out = jnp.einsum('enh,ehd->end', h, w2) + b2[:, None, :]
        routing_output = expert_out.sum(axis=0)
        shared = jax.nn.relu(xf @ sw1 + sb1) @ sw2 + sb2
        return (routing_output + shared).reshape(B, S, D)

    def _L1_attn_ref(x, W_qkv, W_o):
        import math
        import jax, jax.numpy as jnp
        import numpy as np
        D = 128
        NH = 16
        DH = D // NH

        def _rope(q, k, base=10000.0):
            half = q.shape[-1] // 2
            freqs = jnp.arange(half, dtype=q.dtype) / half
            theta = 1.0 / base ** freqs
            t = jnp.arange(q.shape[-2], dtype=q.dtype)
            ang = t[:, None] * theta[None, :]
            cos = jnp.cos(ang)[None, None, :, :]
            sin = jnp.sin(ang)[None, None, :, :]

            def rot(x):
                x1, x2 = (x[..., :half], x[..., half:])
                return jnp.concatenate([x1 * cos - x2 * sin, x1 * sin + x2 * cos], axis=-1)
            return (rot(q), rot(k))
        B, T, d = x.shape
        qkv = x @ W_qkv
        q, k, v = jnp.split(qkv, 3, axis=-1)
        q = q.reshape(B, T, NH, DH).transpose(0, 2, 1, 3)
        k = k.reshape(B, T, NH, DH).transpose(0, 2, 1, 3)
        v = v.reshape(B, T, NH, DH).transpose(0, 2, 1, 3)
        q, k = _rope(q, k)
        att = jnp.einsum('bhtd,bhsd->bhts', q, k) / math.sqrt(DH)
        mask = jnp.triu(jnp.full((T, T), -jnp.inf, dtype=att.dtype), 1)
        att = att + mask
        w = jax.nn.softmax(att, axis=-1)
        y = jnp.einsum('bhts,bhsd->bhtd', w, v)
        y = y.transpose(0, 2, 1, 3).reshape(B, T, d)
        return y @ W_o

    def _L1_ffn_ref(x, Wg, W1, W2, W3):
        import jax, jax.numpy as jnp
        import numpy as np
        B, S, D, F, E, K = (2, 256, 128, 256, 8, 2)
        k = K
        scores = jnp.einsum('bsd,ed->bse', x, Wg)
        topk_scores, topk_idx = jax.lax.top_k(scores, k)
        topk_probs = jax.nn.softmax(topk_scores, axis=-1)
        h1 = jnp.einsum('bsd,efd->bsef', x, W1)
        h2 = jnp.einsum('bsd,efd->bsef', x, W2)
        hidden = jax.nn.silu(h1) * h2
        expert_out = jnp.einsum('bsef,edf->bsed', hidden, W3)
        onehot = jax.nn.one_hot(topk_idx, scores.shape[-1], dtype=x.dtype)
        gating = jnp.einsum('bsk,bske->bse', topk_probs, onehot)
        return jnp.einsum('bse,bsed->bsd', gating, expert_out)
    x = L0_attn_hidden_states
    x = _layernorm(x + _L0_attn_ref(x, L0_attn_Wq, L0_attn_Wk, L0_attn_Wv, L0_attn_Wo, L0_attn_g_weight), axis=-1)
    x = _layernorm(x + _L0_ffn_ref(x, L0_ffn_gate_w, L0_ffn_w1, L0_ffn_b1, L0_ffn_w2, L0_ffn_b2, L0_ffn_sw1, L0_ffn_sb1, L0_ffn_sw2, L0_ffn_sb2), axis=-1)
    x = _layernorm(x + _L1_attn_ref(x, L1_attn_W_qkv, L1_attn_W_o), axis=-1)
    x = _layernorm(x + _L1_ffn_ref(x, L1_ffn_Wg, L1_ffn_W1, L1_ffn_W2, L1_ffn_W3), axis=-1)
    return x

_drawn_inputs = setup_inputs


def setup_inputs(seed=0):
    import zlib

    import numpy as np

    out = dict(_drawn_inputs(seed))
    spreads = {'L0_attn_g_weight': (1.0, 0.2)}
    factors = {'L0_ffn_b1': 6.127,
     'L0_ffn_sb1': 8.0,
     'L1_ffn_Wg': 8.0,
     'L1_ffn_W1': 8.0,
     'L1_ffn_W2': 8.0,
     'L1_ffn_W3': 8.0}
    for name, (base, spread) in spreads.items():
        noise = np.random.default_rng([zlib.crc32(name.encode()), seed]).standard_normal(out[name].shape)
        drawn = base * np.exp(spread * noise) if base else spread * noise
        out[name] = jnp.asarray(drawn.astype(out[name].dtype))
    for name, factor in factors.items():
        out[name] = (out[name] * factor).astype(out[name].dtype)
    return out
```

```python
from contextlib import ExitStack

import numpy as np
import concourse.bass as bass
from concourse import mybir

F32 = mybir.dt.float32
F32R = mybir.dt.float32r
BF16 = mybir.dt.bfloat16
U32 = mybir.dt.uint32
ACT = mybir.ActivationFunctionType
ALU = mybir.AluOpType
AX = mybir.AxisListType

P = 128
D = 128
NB, L = 8, 256
N = NB * L
NT = N // P
LN_EPS = 1e-5
H0, FD, E0 = 16, 16, 64
NPAIR = H0 // 2
RMS_EPS = 1e-5
SW = 384
HID, NE0 = 512, 3
HC = HID // P
H1, D1 = 16, 8
NE1, F1 = 8, 256
FC1 = F1 // P
BT = 512
NBLK = N // BT


def dma_in(eng, dst, src, done):
    eng.dma_start(dst, src).then_inc(done, 16)


def three_pass(pe, out, a_hi, a_lo, b_hi, b_lo):
    pe.matmul(out, a_hi, b_hi, start=True, stop=False)
    pe.matmul(out, a_lo, b_hi, start=False, stop=False)
    return pe.matmul(out, a_hi, b_lo, start=False, stop=True)


def lagged(b, v, j, lag=2):
    if not 0 <= v * NPAIR + j - lag < NB * NPAIR:
        return None
    return (b, v, j - lag) if j >= lag else (b - 1, v - 1, j - lag + NPAIR)


def attention0(nc, mem, dr):
    X, RES = mem["X"], mem["RES"]
    ctx = ExitStack()
    with ctx:
        sb = lambda n, s, d=F32: ctx.enter_context(nc.sbuf_tensor(n, s, d))
        sem = lambda n: ctx.enter_context(nc.semaphore(n))
        xT = sb("a0_xT", [P, N])
        w_qk = sb("a0_wqk", [P, 4, P])
        w_v = sb("a0_wv", [P, H0 * E0])
        qk_h = sb("a0_wqk_h", [P, 4, P], F32R)
        qk_l = sb("a0_wqk_l", [P, 4, P], F32R)
        v_h = sb("a0_wv_h", [P, H0 * E0], F32R)
        v_l = sb("a0_wv_l", [P, H0 * E0], F32R)
        w_o = sb("a0_wo", [P, NPAIR, D])
        w_og = sb("a0_wog", [P, NPAIR, D])
        g_col = sb("a0_g", [P, 1])
        mask = sb("a0_mask", [P, SW])
        sum_sel = sb("a0_sumsel", [P, NPAIR, 32])
        exp_selw = sb("a0_expselw", [P, NPAIR, P])
        exp_sel = sb("a0_expsel", [P, NPAIR, P], F32R)
        neg_half = sb("a0_neghalf", [P, 2])
        one_col = sb("a0_one", [P, 1])
        warm = sb("a0_warm", [P, 1])
        xs_h = sb("a0_xs_h", [P, 2, L], F32R)
        xs_l = sb("a0_xs_l", [P, 2, L], F32R)
        c_h = sb("a0_c_h", [P, 2, 2 * L], F32R)
        c_l = sb("a0_c_l", [P, 2, 2 * L], F32R)
        q4 = sb("a0_q4", [P, 2, NPAIR * L], F32R)
        k4 = sb("a0_k4", [P, 2, NPAIR * L], F32R)
        V = sb("a0_V", [P, 2, 2, H0 * E0])
        UA = sb("a0_UA", [P, 4, 2, SW])
        Y = sb("a0_Y", [P, 2, NPAIR, L])
        Y2 = sb("a0_Y2", [P, 2, NPAIR, L])
        YN = sb("a0_YN", [P, NPAIR, L])
        ms = sb("a0_ms", [P, L])
        rms = sb("a0_rms", [P, L])
        rr = sb("a0_rr", [P, L])
        rr_h = sb("a0_rr_h", [P, L], F32R)
        rr_l = sb("a0_rr_l", [P, L], F32R)
        st = sb("a0_st", [P, 2, 6])
        mv = sb("a0_mv", [P, 2, 2])
        ve = sb("a0_ve", [P, 2])
        rs = sb("a0_rs", [P, 2])
        S = [ctx.enter_context(nc.psum_tensor(f"a0_S{i}", [P, 2, 512], F32)) for i in range(2)]
        YP = [ctx.enter_context(nc.psum_tensor(f"a0_Y{i}", [P, 512], F32)) for i in range(2)]
        PJ = ctx.enter_context(nc.psum_tensor("a0_PJ", [P, 512], F32))
        MI = ctx.enter_context(nc.psum_tensor("a0_MI", [P, 512], F32))

        in_x0, in_x1, in_x, in_wqk, in_wv, in_mask, in_c, in_res, in_g, in_o = (sem(f"a0_in_{n}") for n in "x0 x1 x wqk wv mask c res g o".split())
        w_split = sem("a0_w_split")
        consts = sem("a0_consts")
        xs_hi = sem("a0_xs_hi")
        xs_ready = sem("a0_xs_ready")
        pj_ready = sem("a0_pj_ready")
        pj_read = sem("a0_pj_read")
        hi_ready = sem("a0_hi_ready")
        lo_ready = sem("a0_lo_ready")
        stacked = sem("a0_stacked")
        s_ready = sem("a0_s_ready")
        sq_done = sem("a0_sq_done")
        a_ready = sem("a0_a_ready")
        y_ready = sem("a0_y_ready")
        y_copied = sem("a0_y_copied")
        y2_ready = sem("a0_y2_ready")
        mi_ready = sem("a0_mi_ready")
        mi_read = sem("a0_mi_read")
        rr_ready = sem("a0_rr_ready")
        rms_ready = sem("a0_rms_ready")
        rr_hi = sem("a0_rr_hi")
        rr_split = sem("a0_rr_split")
        ln_step = sem("a0_ln_step")
        ve_ready = sem("a0_ve_ready")
        rs_ready = sem("a0_rs_ready")
        x_done = sem("a0_x_done")
        w_step = sem("a0_w_step")
        warm_done = sem("a0_warm_done")

        def spread_at(b, v, j):
            if j >= 5 and 1 <= v <= NB:
                return b, v, j - 5
            return (b - 1, v - 1, 3) if j == 0 and v >= 2 else None

        def proj_bank(v, u):
            return (S[0][:, 0, :], S[0][:, 1, :], S[1][:, 0, :], S[1][:, 1, :], YP[0], YP[1], MI, PJ)[u] if v == 0 else PJ

        def spread_bank(v, g):
            return S[g // 2][:, g % 2, :] if v == NB else MI[:, :]

        MI_OF = lambda b: 5 + 6 * (b - 2)

        block = ctx.enter_context(nc.Block())

        @block.sync
        def _(sp):
            dma_in(sp, w_qk[:, :, :], dr["a0_wqk"], in_wqk)
            dma_in(sp, xT[:, 0:L], dr["xT"][:, 0:L], in_x0)
            dma_in(sp, w_v[:, :], dr["a0_wv"], in_wv)
            dma_in(sp, mask[:, :], dr["mask0"], in_mask)
            dma_in(sp, xT[:, L:2 * L], dr["xT"][:, L:2 * L], in_x1)

            def stack(b, v, par):
                for t, (dst, parts) in enumerate(((q4, (c_h, c_h, c_l, c_l)), (k4, (c_h, c_l, c_h, c_l)))):
                    sp.wait_ge(lo_ready, b * 4 + 2 * t + 2)
                    if v >= 2 and t == 0:
                        sp.wait_ge(s_ready, (b - 1) * NPAIR)
                    for c in range(4):
                        sp.dma_start(dst[c:P:4, par, :].bitcast(F32), parts[c][:, t, :].bitcast(F32)).then_inc(stacked, 16)

            stack(0, 0, 0)
            dma_in(sp, sum_sel[:, :, :], dr["sum_sel"], in_c)
            dma_in(sp, exp_selw[:, :, :], dr["exp_sel"], in_c)
            dma_in(sp, xT[:, 2 * L:N], dr["xT"][:, 2 * L:N], in_x)
            dma_in(sp, w_o[:, :, :], dr["a0_wo"], in_o)
            dma_in(sp, g_col[:, :], dr["a0_g"], in_g)
            dma_in(sp, X[:, :, :], dr["x"], in_res)
            stack(1, 1, 1)
            mem["load_later"](sp)
            for b in range(2, NB):
                stack(b, b, b % 2)
            mem["wait_later"](sp)

        @block.gpsimd
        def _(pool):
            pool.memset(neg_half[:, :], -0.5).then_inc(consts, 1)
            pool.memset(one_col[:, :], 1.0).then_inc(consts, 1)
            pool.sem_inc(sq_done, 2)
            pool.sem_inc(y_ready, 4)
            pool.sem_inc(y_copied, 2)

            def split_x(b, v, par):
                pool.wait_ge((in_x0, in_x1)[v] if v < 2 else in_x, 16)
                if v >= 2:
                    pool.wait_ge(pj_ready, (b - 1) * 8)
                src = xT[:, bass.ds(b * L, L)] if not isinstance(b, int) else xT[:, b * L:(b + 1) * L]
                pool.tensor_scalar(xs_h[:, par, :], src, 1.0, 0.0, ALU.mult, ALU.add).then_inc(xs_hi, 1)
                pool.wait_ge(xs_hi, b + 1)
                pool.tensor_tensor(xs_l[:, par, :], src, xs_h[:, par, :].bitcast(F32), ALU.subtract).then_inc(xs_ready, 1)

            split_x(0, 0, 0)
            split_x(1, 1, 1)

            def square(b, v, j):
                n = b * NPAIR + j
                pool.wait_ge(y_copied, n + 1 + 2)
                if v >= 2 and j == 0:
                    pool.wait_ge(mi_ready, MI_OF(b) - 4 if v > 2 else 1)
                pool.tensor_tensor(Y2[:, v % 2, j, :], Y[:, v % 2, j, :], Y[:, v % 2, j, :], ALU.mult).then_inc(y2_ready, 1)

            def step(b, v):
                for j in range(NPAIR):
                    if lagged(b, v, j):
                        square(*lagged(b, v, j))
                    if j == 2 and 2 <= v:
                        pool.wait_ge(ve_ready, b - 1)
                        pool.tensor_tensor(rs[:, :], ve[:, :], neg_half[:, 0:2], ALU.pow).then_inc(rs_ready, 1)
                    if j == 6 and v + 2 < NB:
                        split_x(b + 2, v + 2, v % 2)

            for b in range(NB + 2):
                step(b, b)
                if b == 0:
                    pool.wait_ge(in_o, 16)
                    pool.wait_ge(in_g, 16)
                    pool.tensor_scalar(w_og[:, :, :], w_o[:, :, :], g_col[:, 0:1], 1.0, ALU.mult, ALU.mult).then_inc(consts, 1)
                if b in (3, 4, 5):
                    if b == 3:
                        pool.wait_ge(mem["in_w1"], 16)
                    e = b - 3
                    split_on_pool(pool, mem["w1"][:, e, :], mem["w1_h"][:, e, :], mem["w1_l"][:, e, :], w_step, e, mem["w_split"])

        @block.scalar
        def _(act):
            def evacuate(b, v, u):
                act.wait_ge(pj_ready, b * 8 + u + 1)
                if u < 4:
                    if u == 0 and v >= 1:
                        act.wait_ge(stacked, 128 * b)
                    act.activation(c_h[:, u // 2, (u % 2) * L:(u % 2 + 1) * L], proj_bank(v, u)[:, 0:L], ACT.Copy).then_inc(hi_ready, 1)
                else:
                    t, half = divmod(u - 4, 2)
                    act.activation(V[:, v % 2, t, half * 512:(half + 1) * 512], proj_bank(v, u)[:, :], ACT.Copy).then_inc(pj_read, 1)

            def copy_y(b, v, j):
                act.wait_ge(y_ready, b * NPAIR + j + 1 + 4)
                act.activation(Y[:, v % 2, j, :], YP[j % 2][:, 0:L], ACT.Copy).then_inc(y_copied, 1)

            def step(b, v):
                for j in range(NPAIR):
                    if v < NB:
                        n = b * NPAIR + j
                        act.wait_ge(s_ready, n + 1)
                        act.wait_ge(y_ready, n + 1)
                        act.activation(UA[:, j % 4, :, :], S[j % 2][:, :, 0:SW], ACT.Square,
                                       bias=one_col[:, 0:1], scale=0.25).then_inc(sq_done, 1)
                    if j == 3 and 1 <= v <= NB:
                        act.wait_ge(mi_read, MI_OF(b) + 2 if v > 1 else 1)
                        act.activation(rms[:, :], ms[:, :], ACT.Sqrt).then_inc(rms_ready, 1)
                    if lagged(b, v, j):
                        copy_y(*lagged(b, v, j))
                    if v + 1 < NB:
                        evacuate(b + 1, v + 1, j)

            act.wait_ge(consts, 2)
            act.activation(warm[:, :], one_col[:, :], ACT.Square).then_inc(warm_done, 1)
            for u in range(8):
                evacuate(0, 0, u)
            for b in range(NB + 1):
                step(b, b)

        @block.vector
        def _(dve):
            for n, (w, h, l, loaded) in enumerate(((w_qk, qk_h, qk_l, in_wqk), (w_v, v_h, v_l, in_wv))):
                dve.wait_ge(loaded, 16)
                full = (slice(None),) * len(w.shape)
                dve.tensor_copy(h[full], w[full]).then_inc(w_split, 1)
                dve.wait_ge(w_split, 2 * n + 1)
                dve.tensor_tensor(l[full], w[full], h[full].bitcast(F32), ALU.subtract).then_inc(w_split, 1)

            def low(b, v, u):
                dve.wait_ge(hi_ready, b * 4 + u + 1)
                out = slice((u % 2) * L, (u % 2 + 1) * L)
                dve.tensor_tensor(c_l[:, u // 2, out], proj_bank(v, u)[:, 0:L], c_h[:, u // 2, out].bitcast(F32),
                                  ALU.subtract).then_inc(lo_ready, 1)

            def norm(b, v):
                e = MI_OF(b + 2)
                dve.wait_ge(mi_ready, e + 1)
                if v == 0:
                    dve.wait_ge(in_res, 16)
                x = X[:, 2 * b:2 * b + 2, :] if isinstance(b, int) else X[:, bass.ds(2 * b, 2), :]
                dve.tensor_tensor(RES[:, v % 2, :, :], MI[:, 0:2 * D].rearrange("p (t d) -> p t d", t=2), x, ALU.add).then_inc(mi_read, 1)
                dve.wait_ge(mi_read, e + 1)
                for t in range(2):
                    i = dve.bn_stats(st[:, t, :], RES[:, v % 2, t, :])
                i.then_inc(ln_step, 1)
                dve.wait_ge(ln_step, 2 * b + 1)
                for t in range(2):
                    i = dve.bn_aggr(mv[:, t, :], st[:, t, :])
                i.then_inc(ln_step, 1)
                dve.wait_ge(ln_step, 2 * b + 2)
                dve.tensor_scalar(ve[:, :], mv[:, :, 1], LN_EPS, None, ALU.add).then_inc(ve_ready, 1)

            def norm_end(b, v):
                dve.wait_ge(rs_ready, b + 1)
                for t in range(2):
                    out = X[:, 2 * b + t, :]
                    i = dve.tensor_scalar(out, RES[:, v % 2, t, :], mv[:, t, 0:1], rs[:, t:t + 1], ALU.subtract, ALU.mult)
                i.then_inc(x_done, 1)

            def scale(b, v, g):
                e = MI_OF(b) + 2 + g if v > 1 else 1 + g
                dve.wait_ge(mi_ready, e + 1)
                dve.tensor_tensor(YN[:, 2 * g:2 * g + 2, :], spread_bank(v, g).rearrange("p (j n) -> p j n", j=2),
                                  Y[:, (v - 1) % 2, 2 * g:2 * g + 2, :], ALU.mult).then_inc(mi_read, 1)

            def step(b, v):
                for j in range(NPAIR):
                    if j == 3 and 1 <= v <= NB:
                        e = MI_OF(b) + 1 if v > 1 else 0
                        dve.wait_ge(mi_ready, e + 1)
                        dve.tensor_scalar(ms[:, :], MI[:, 0:L], 1.0 / E0, 4 * RMS_EPS, ALU.mult, ALU.add).then_inc(mi_read, 1)
                    if j == 4 and 1 <= v <= NB:
                        dve.wait_ge(rms_ready, b)
                        dve.reciprocal(rr[:, :], rms[:, :]).then_inc(rr_ready, 1)
                        dve.wait_ge(rr_ready, b)
                        dve.tensor_copy(rr_h[:, :], rr[:, :]).then_inc(rr_hi, 1)
                        dve.wait_ge(rr_hi, b)
                        dve.tensor_tensor(rr_l[:, :], rr[:, :], rr_h[:, :].bitcast(F32), ALU.subtract).then_inc(rr_split, 1)
                    if v < NB:
                        n = b * NPAIR + j
                        dve.wait_ge(sq_done, n + 1 + 2)
                        dve.scalar_tensor_tensor(UA[:, j % 4, :, :], UA[:, j % 4, :, :], 1.0,
                                                 mask[:, None, :].to_broadcast([P, 2, SW]), ALU.add, ALU.mult).then_inc(a_ready, 1)
                    if v + 1 < NB and j < 4:
                        low(b + 1, v + 1, j)
                    if j == 1 and v >= 2:
                        norm(b - 2, v - 2)
                    if j == 3 and v >= 2:
                        norm_end(b - 2, v - 2)
                    if spread_at(b, v, j):
                        scale(*spread_at(b, v, j))

            for u in range(4):
                low(0, 0, u)
            dve.wait_ge(in_mask, 16)
            for b in range(NB + 2):
                step(b, b)
                if b == 0:
                    dve.wait_ge(in_c, 32)
                    dve.tensor_copy(exp_sel[:, :, :], exp_selw[:, :, :]).then_inc(w_split, 1)

        @block.tensor
        def _(pe):
            def project(b, v, u):
                if u == 0:
                    pe.wait_ge(xs_ready, b + 1)
                if v == 0:
                    pe.wait_ge(w_split, 2 if u < 4 else 4)
                elif u == 0:
                    pe.wait_ge(pj_read, 4 * b)
                elif u <= 4:
                    pe.wait_ge(lo_ready, 4 * b + u)
                else:
                    pe.wait_ge(pj_read, 4 * b + u - 4)
                xh, xl = xs_h[:, v % 2, :], xs_l[:, v % 2, :]
                if u < 4:
                    i = three_pass(pe, proj_bank(v, u)[:, 0:L], qk_h[:, u, :], qk_l[:, u, :], xh, xl)
                else:
                    t, half = divmod(u - 4, 2)
                    tt, hh = slice(t * P, (t + 1) * P), slice(half * 512, (half + 1) * 512)
                    i = three_pass(pe, proj_bank(v, u)[:, :], xs_h[:, v % 2, tt], xs_l[:, v % 2, tt], v_h[:, hh], v_l[:, hh])
                i.then_inc(pj_ready, 1)

            def scores(b, v, j):
                n = b * NPAIR + j
                if j == 0:
                    pe.wait_ge(stacked, 128 * (b + 1))
                pe.wait_ge(sq_done, n + 1)
                for par in range(2):
                    rows = slice(64 * par, 64 * par + 64)
                    kk, qq = k4[rows, v % 2, j * L:(j + 1) * L], q4[rows, v % 2, j * L:(j + 1) * L]
                    pe.matmul(S[j % 2][:, par, 0:L], kk[:, 0:P], qq[:, 0:L], start=True, stop=True)
                    i = pe.matmul(S[j % 2][:, par, L:SW], kk[:, P:L], qq[:, P:L], start=True, stop=True)
                i.then_inc(s_ready, 1)

            def attend(b, v, j):
                n = b * NPAIR + j
                pe.wait_ge(a_ready, n + 1)
                pe.wait_ge(y_copied, n + 1)
                if n == 0:
                    pe.wait_ge(pj_read, 4)
                for t in range(2):
                    for par in range(2):
                        h = 2 * j + par
                        cols = slice(0, L) if t == 0 else slice(L, SW)
                        i = pe.matmul(YP[j % 2][64 * par:64 * par + 64, t * P:L], V[:, v % 2, t, h * E0:(h + 1) * E0],
                                      UA[:, j % 4, par, cols], start=(t == 0), stop=(t == 1), skip_group_check=True)
                i.then_inc(y_ready, 1)

            def spread(b, v, g):
                if v < NB:
                    pe.wait_ge(mi_read, MI_OF(b) + 2 + g if v > 1 else 1 + g)
                else:
                    pe.wait_ge(sq_done, NB * NPAIR + 2)
                if g == 0:
                    pe.wait_ge(rr_split, b)
                if v == 1 and g == 0:
                    pe.wait_ge(w_split, 5)
                for k in range(2):
                    out = spread_bank(v, g)[:, k * L:(k + 1) * L]
                    pe.matmul(out, exp_sel[:, 2 * g + k, :], rr_h[:, :], start=(k == 0), stop=False, skip_group_check=True)
                    i = pe.matmul(out, exp_sel[:, 2 * g + k, :], rr_l[:, :], start=False, stop=True, skip_group_check=True)
                i.then_inc(mi_ready, 1)

            def step(b, v):
                for j in range(NPAIR):
                    if v < NB:
                        scores(b, v, j)
                    if lagged(b, v, j):
                        attend(*lagged(b, v, j))
                    if spread_at(b, v, j):
                        spread(*spread_at(b, v, j))
                    if v + 1 < NB:
                        project(b + 1, v + 1, j)
                    if j == 1 and v >= 2:
                        if v == 2:
                            pe.wait_ge(consts, 3)
                        pe.wait_ge(mi_read, MI_OF(b))
                        for t in range(2):
                            for k in range(NPAIR):
                                i = pe.matmul(MI[:, t * D:(t + 1) * D], YN[:, k, t * P:(t + 1) * P], w_og[:, k, :],
                                              start=(k == 0), stop=(k == NPAIR - 1))
                        i.then_inc(mi_ready, 1)
                    if j == 2 and 1 <= v <= NB:
                        e = MI_OF(b) + 1 if v > 1 else 0
                        pe.wait_ge(mi_read, e)
                        pe.wait_ge(y2_ready, b * NPAIR)
                        for k in range(NPAIR):
                            q = 32 * (k % 4)
                            i = pe.matmul(MI[q:q + 32, 0:L], sum_sel[:, k, :], Y2[:, (v - 1) % 2, k, :],
                                          start=(k < 4), stop=(k >= 4), skip_group_check=True)
                        i.then_inc(mi_ready, 1)
            for u in range(8):
                project(0, 0, u)
            for b in range(NB + 2):
                step(b, b)


def norm_stats(dve, res, stats, mv, var, tiles, step, done, ready):
    for t in range(tiles):
        i = dve.bn_stats(stats[:, t, :], res[:, t, :])
    i.then_inc(step, 1)
    dve.wait_ge(step, done + 1)
    for t in range(tiles):
        i = dve.bn_aggr(mv[:, t, :], stats[:, t, :])
    i.then_inc(step, 1)
    dve.wait_ge(step, done + 2)
    dve.tensor_scalar(var[:, 0:tiles], mv[:, 0:tiles, 1], LN_EPS, None, ALU.add).then_inc(ready, 1)


def norm_apply(dve, out, res, mv, rstd, tiles):
    for t in range(tiles):
        i = dve.tensor_scalar(out[:, t, :], res[:, t, :], mv[:, t, 0:1], rstd[:, t:t + 1], ALU.subtract, ALU.mult)
    return i


def split_on_pool(pool, src, hi, lo, step, done, ready):
    pool.tensor_scalar(hi, src, 1.0, 0.0, ALU.mult, ALU.add).then_inc(step, 1)
    pool.wait_ge(step, done + 1)
    pool.tensor_tensor(lo, src, hi.bitcast(F32), ALU.subtract).then_inc(ready, 1)


def feed_forward0(nc, mem, dr):
    X = mem["X"]
    TB = BT // P
    NC = NE0 * HC
    ctx = ExitStack()
    with ctx:
        sb = lambda n, s, d=F32: ctx.enter_context(nc.sbuf_tensor(n, s, d))
        sem = lambda n: ctx.enter_context(nc.semaphore("f0_" + n))
        w1_h, w1_l, w2 = mem["w1_h"], mem["w1_l"], mem["w2"]
        b1, b2 = mem["b1"], mem["b2"]
        b_sum = sb("f0_bsum", [P, 2, D])
        xb = sb("f0_xb", [P, 2, TB, D])
        xT = sb("f0_xT", [P, TB, P])
        x0 = sb("f0_x0", [P, TB, D])
        pick0 = sb("f0_pick0", [P, 2, TB])
        sc = sb("f0_sc", [P, 2, TB, 2])
        xh = sb("f0_xh", [P, 2, NE0, BT], F32R)
        xl = sb("f0_xl", [P, 2, NE0, BT], F32R)
        hid = sb("f0_hid", [P, 2, NC, BT])
        res = sb("f0_res", [P, 2, TB, D])
        stats = sb("f0_stats", [P, TB, 6])
        mv = sb("f0_mv", [P, 2, TB, 2])
        var = sb("f0_var", [P, TB])
        rstd = sb("f0_rstd", [P, TB])
        neg_half = sb("f0_neghalf", [P, TB])
        T = [ctx.enter_context(nc.psum_tensor(f"f0_T{i}", [P, 512], F32)) for i in range(2)]
        G = ctx.enter_context(nc.psum_tensor("f0_G", [P, 512], F32))
        HP = [ctx.enter_context(nc.psum_tensor(f"f0_H{i}", [P, 512], F32)) for i in range(3)]
        O = [ctx.enter_context(nc.psum_tensor(f"f0_O{i}", [P, 512], F32)) for i in range(2)]
        bias_step, bias_ready, xb_ready = sem("bias_step"), sem("bias_ready"), sem("xb_ready")
        t_ready = sem("t_ready")
        xT_ready = sem("xT_ready")
        gate_ready = sem("gate_ready")
        sc_ready = sem("sc_ready")
        pick_ready = sem("pick_ready")
        x0_ready = sem("x0_ready")
        xh_ready = sem("xh_ready")
        xl_ready = sem("xl_ready")
        x1h_ready, x1l_ready = sem("x1h_ready"), sem("x1l_ready")
        h_ready = sem("h_ready")
        h_act, h_dve = sem("h_act"), sem("h_dve")
        o_ready = sem("o_ready")
        res_ready, ln_step, var_ready, rstd_ready, x_done = (sem(n) for n in "res_ready ln_step var_ready rstd_ready x_done".split())
        consts, split_step = sem("consts"), sem("split_step")
        block = ctx.enter_context(nc.Block())

        @block.sync
        def _(sp):
            mem["load_layer1"](sp)

        @block.gpsimd
        def _(pool):
            pool.memset(neg_half[:, :], -0.5).then_inc(consts, 1)
            pool.tensor_tensor(b_sum[:, 0, :], b2[:, 0, :], b2[:, 1, :], ALU.add).then_inc(bias_step, 1)
            pool.wait_ge(bias_step, 1)
            pool.tensor_tensor(b_sum[:, 1, :], b_sum[:, 0, :], b2[:, 2, :], ALU.add).then_inc(bias_ready, 1)
            pool.wait_ge(bias_ready, 1)
            splits = 0
            for i in range(NBLK):
                p = i % 2
                pool.wait_ge(xl_ready, 2 * i + 2)
                pool.tensor_tensor(xh[:, p, 1, :], xh[:, p, 2, :].bitcast(F32), xh[:, p, 0, :].bitcast(F32), ALU.subtract).then_inc(x1h_ready, 1)
                pool.tensor_tensor(xl[:, p, 1, :], xl[:, p, 2, :].bitcast(F32), xl[:, p, 0, :].bitcast(F32), ALU.subtract).then_inc(x1l_ready, 1)
                if i >= 2:
                    pool.wait_ge(res_ready, i - 1)
                pool.tensor_tensor(xb[:, p, :, :], X[:, TB * i:TB * i + TB, :],
                                   b_sum[:, 1:2, :].to_broadcast([P, TB, D]), ALU.add).then_inc(xb_ready, 1)
                if i >= 2:
                    pool.wait_ge(var_ready, i - 1)
                    pool.tensor_tensor(rstd[:, :], var[:, :], neg_half[:, :], ALU.pow).then_inc(rstd_ready, 1)
                for src, hi, lo, loaded, cols in mem["splits"][i]:
                    pool.wait_ge(loaded, 16)
                    for c in range(0, cols, 512):
                        split_on_pool(pool, src[:, c:c + 512], hi[:, c:c + 512], lo[:, c:c + 512], split_step, splits, mem["w_split"])
                        splits += 1
            for i in range(NBLK - 2, NBLK):
                pool.wait_ge(var_ready, i + 1)
                pool.tensor_tensor(rstd[:, :], var[:, :], neg_half[:, :], ALU.pow).then_inc(rstd_ready, 1)

        @block.scalar
        def _(act):
            def prepare(i, part):
                p = i % 2
                if part == 0:
                    act.wait_ge(t_ready, 2 * i + 1)
                    act.activation(xT[:, :, :], T[0][:, :].rearrange("p (t n) -> p t n", t=TB), ACT.Copy).then_inc(xT_ready, 1)
                    if i >= 2:
                        act.wait_ge(h_ready, (i - 1) * NC)
                    act.activation(xh[:, p, 2, :], T[0][:, :], ACT.Copy).then_inc(xh_ready, 1)
                else:
                    act.wait_ge(t_ready, 2 * i + 2)
                    act.activation(xh[:, p, 0, :], T[1][:, :], ACT.Copy).then_inc(xh_ready, 1)

            prepare(0, 0)
            prepare(0, 1)
            for i in range(NBLK):
                for c in range(0, NC, 2):
                    act.wait_ge(h_ready, i * NC + c + 1)
                    if i >= 2 and c == 0:
                        act.wait_ge(o_ready, i - 1)
                    act.activation(hid[:, i % 2, c, :], HP[(i * NC + c) % 3][:, :], ACT.Relu, bias=b1[:, c:c + 1]).then_inc(h_act, 1)
                    if i + 1 < NBLK and c in (2, 8):
                        prepare(i + 1, (c - 2) // 6)

        @block.vector
        def _(dve):
            def prepare(i, part):
                p = i % 2
                if part == 0:
                    dve.wait_ge(xh_ready, 2 * i + 1)
                    dve.tensor_tensor(xl[:, p, 2, :], T[0][:, :], xh[:, p, 2, :].bitcast(F32), ALU.subtract).then_inc(xl_ready, 1)
                    dve.wait_ge(gate_ready, i + 1)
                    dve.tensor_copy(sc[:, p, :, :], G[:, 0:2 * TB].rearrange("p (t e) -> p t e", e=2)).then_inc(sc_ready, 1)
                    dve.wait_ge(sc_ready, i + 1)
                    dve.tensor_tensor(pick0[:, p, :], sc[:, p, :, 0], sc[:, p, :, 1], ALU.is_ge).then_inc(pick_ready, 1)
                    dve.wait_ge(pick_ready, i + 1)
                    for t in range(TB):
                        k = dve.tensor_scalar(x0[:, t, :], X[:, TB * i + t, :], pick0[:, p, t:t + 1], None, ALU.mult)
                    k.then_inc(x0_ready, 1)
                else:
                    dve.wait_ge(xh_ready, 2 * i + 2)
                    dve.tensor_tensor(xl[:, p, 0, :], T[1][:, :], xh[:, p, 0, :].bitcast(F32), ALU.subtract).then_inc(xl_ready, 1)

            def residual(i):
                dve.wait_ge(o_ready, i + 1)
                dve.wait_ge(xb_ready, i + 1)
                dve.tensor_tensor(res[:, i % 2, :, :], O[i % 2][:, :].rearrange("p (t d) -> p t d", t=TB), xb[:, i % 2, :, :], ALU.add).then_inc(res_ready, 1)
                dve.wait_ge(res_ready, i + 1)
                norm_stats(dve, res[:, i % 2], stats, mv[:, i % 2], var, TB, ln_step, 2 * i, var_ready)

            def finish(i):
                dve.wait_ge(rstd_ready, i + 1)
                norm_apply(dve, X[:, TB * i:TB * i + TB, :], res[:, i % 2], mv[:, i % 2], rstd, TB).then_inc(x_done, 1)

            prepare(0, 0)
            prepare(0, 1)
            for i in range(NBLK + 1):
                for c in range(1, NC, 2):
                    if i < NBLK:
                        dve.wait_ge(h_ready, i * NC + c + 1)
                        dve.tensor_scalar(hid[:, i % 2, c, :], HP[(i * NC + c) % 3][:, :], b1[:, c:c + 1], 0.0, ALU.add, ALU.max).then_inc(h_dve, 1)
                    if i + 1 < NBLK and c in (3, 9):
                        prepare(i + 1, (c - 3) // 6)
                    if c == 1 and i >= 2:
                        residual(i - 2)
                    if c == 7 and i >= 2:
                        finish(i - 2)
            residual(NBLK - 1)
            finish(NBLK - 1)

        @block.tensor
        def _(pe):
            def prepare(i, part):
                if part == 0:
                    if i >= 1:
                        pe.wait_ge(xl_ready, 2 * i - 1)
                    for t in range(TB):
                        k = pe.transpose(T[0][:, t * P:(t + 1) * P], X[:, TB * i + t, :], mem["ident"][:, :])
                    k.then_inc(t_ready, 1)
                elif part == 1:
                    pe.wait_ge(xT_ready, i + 1)
                    if i >= 1:
                        pe.wait_ge(sc_ready, i)
                    for t in range(TB):
                        k = pe.matmul(G[:, 2 * t:2 * t + 2], xT[:, t, :], mem["gate_w"][:, :], start=True, stop=True)
                    k.then_inc(gate_ready, 1)
                else:
                    pe.wait_ge(x0_ready, i + 1)
                    if i >= 1:
                        pe.wait_ge(xl_ready, 2 * i)
                    for t in range(TB):
                        k = pe.transpose(T[1][:, t * P:(t + 1) * P], x0[:, t, :], mem["ident"][:, :])
                    k.then_inc(t_ready, 1)

            def up(i, c):
                n, e, p = i * NC + c, c // HC, i % 2
                if n >= 3:
                    pe.wait_ge(h_act if (n - 3) % 2 == 0 else h_dve, (n - 3) // 2 + 1)
                if c == 0:
                    pe.wait_ge(xl_ready, 2 * i + 2)
                if e == 1 and c % HC == 0:
                    pe.wait_ge(x1l_ready, i + 1)
                    pe.wait_ge(x1h_ready, i + 1)
                cols = slice((c % HC) * P, (c % HC + 1) * P)
                three_pass(pe, HP[n % 3][:, :], w1_h[:, e, cols], w1_l[:, e, cols], xh[:, p, e, :], xl[:, p, e, :]).then_inc(h_ready, 1)

            def down(i, s):
                t, third = divmod(s, 3)
                if s == 0 and i >= 2:
                    pe.wait_ge(res_ready, i - 1)
                if s < 3:
                    pe.wait_ge(h_act, i * NC // 2 + 2 * (third + 1))
                    pe.wait_ge(h_dve, i * NC // 2 + 2 * (third + 1))
                for c in range(4 * third, 4 * third + 4):
                    k = pe.matmul(O[i % 2][:, t * D:(t + 1) * D], hid[:, i % 2, c, t * P:(t + 1) * P], w2[:, c, :],
                                  start=(c == 0), stop=(c == NC - 1))
                if s == NC - 1:
                    k.then_inc(o_ready, 1)

            prepare(0, 0)
            prepare(0, 1)
            prepare(0, 2)
            for i in range(NBLK + 1):
                for c in range(NC):
                    if i < NBLK:
                        up(i, c)
                    if i >= 1:
                        down(i - 1, c)
                    if i + 1 < NBLK and c in (2, 5, 8):
                        prepare(i + 1, (c - 2) // 3)


def attention1(nc, mem, dr):
    X = mem["X"]
    NH = NB * H1
    AHEAD = 24
    BUFS = 4
    ctx = ExitStack()
    with ctx:
        sb = lambda n, s, d=F32: ctx.enter_context(nc.sbuf_tensor("a1_" + n, s, d))
        sem = lambda n: ctx.enter_context(nc.semaphore("a1_" + n))
        ident = mem["ident"]
        xT = sb("xT", [P, 2, L])
        xh = sb("xh", [P, 2, L], F32R)
        xl = sb("xl", [P, 2, L], F32R)
        ra = sb("ra", [P, 2, L])
        rb = sb("rb", [P, 2, L])
        rq = sb("rq", [P, 2, L])
        c_h = sb("c_h", [P, 2, L], F32R)
        c_l = sb("c_l", [P, 2, L], F32R)
        q4 = sb("q4", [P, BUFS, NPAIR * L], F32R)
        k4 = sb("k4", [P, BUFS, NPAIR * L], F32R)
        zero_rows = sb("zero_rows", [32, L])
        neg_rows = sb("neg_rows", [32, L])
        V1 = sb("V1", [P, 4, 2, H1, 32])
        m3 = sb("m3", [P, 2, H1, 3])
        mm = sb("mm", [P, 2, H1])
        mx = sb("mx", [P, 2, 2, 2, NPAIR], F32R)
        mT = sb("mT", [32, L], F32R)
        PT = mem["f1_w"][:, 0:8 * SW].rearrange("p (h n) -> p h n", n=SW)
        Yq = sb("Yq", [P, 2, L])
        rden = sb("rden", [P, 2, 4])
        yn = sb("yn", [P, 2, 2, D])
        yT = sb("yT", [P, L])
        res = mem["RES"]
        stats = sb("stats", [P, 2, 6])
        mv = sb("mv", [P, 2, 2, 2])
        var = sb("var", [P, 2])
        rstd = sb("rstd", [P, 2])
        neg_half = sb("neghalf", [P, 2])
        S = [ctx.enter_context(nc.psum_tensor(f"a1_S{i}", [P, 512], F32)) for i in range(2)]
        ST = [ctx.enter_context(nc.psum_tensor(f"a1_ST{i}", [P, 512], F32)) for i in range(2)]
        YP = ctx.enter_context(nc.psum_tensor("a1_YP", [P, 512], F32))
        PJ = ctx.enter_context(nc.psum_tensor("a1_PJ", [P, 512], F32))
        TR = ctx.enter_context(nc.psum_tensor("a1_TR", [P, 512], F32))
        MI = ctx.enter_context(nc.psum_tensor("a1_MI", [P, 512], F32))

        consts, ones_step = sem("consts"), sem("ones_step")
        fixed = sem("fixed")
        xt_ready = sem("xt_ready")
        xT_ready, xh_ready, xl_ready = sem("xT_ready"), sem("xh_ready"), sem("xl_ready")
        pj_ready = sem("pj_ready")
        pj_read = sem("pj_read")
        ra_ready = sem("ra_ready")
        rb_ready = sem("rb_ready")
        rq_ready, ch_ready, cl_ready = sem("rq_ready"), sem("ch_ready"), sem("cl_ready")
        stacked = sem("stacked")
        s_ready, max_done = sem("s_ready"), sem("max_done")
        mm_ready = sem("mm_ready")
        mxh_ready, mx_ready = sem("mxh_ready"), sem("mx_ready")
        mt_ready, mT_ready = sem("mt_ready"), sem("mT_ready")
        m_rows = sem("m_rows")
        st_ready, e_ready, p_ready = sem("st_ready"), sem("e_ready"), sem("p_ready")
        y_ready, yq_ready = sem("y_ready"), sem("yq_ready")
        yt_ready, den_ready, yn_ready = sem("yt_ready"), sem("den_ready"), sem("yn_ready")
        z_ready, yT_ready = sem("z_ready"), sem("yT_ready")
        o_ready = sem("o_ready")
        res_ready, ln_step, var_ready, rstd_ready, x_done = (sem(n) for n in "res_ready ln_step var_ready rstd_ready x_done".split())
        block = ctx.enter_context(nc.Block())

        PREP = {0: "x", 4: "q", 8: "k", 17: "v"}
        PREP_AHEAD = AHEAD + 20
        MAX = 4
        AV, TQ, ZT, OUT = 3, 6, 15, 18
        HASTE = 7
        FIRST, LAST = -PREP_AHEAD, NH + OUT + 3 - HASTE

        def prep_at(g, lag=0):
            for at, k in PREP.items():
                b, off = divmod(g + PREP_AHEAD - lag - at, H1)
                if off == 0 and 0 <= b < NB:
                    return b, k
            return None, ""

        def scores_at(g):
            return g + AHEAD if 0 <= g + AHEAD < NH else None

        def maxima_at(g, lag=MAX):
            b, k = divmod(g + AHEAD - (H1 - 1) - lag, H1)
            return b if k == 0 and 0 <= b < NB else None

        def head_at(g):
            return g if 0 <= g < NH else None

        def quad_at(g, lag):
            q, k = divmod(g - 3 - lag, 4)
            return q if k == 0 and 0 <= q < NH // 4 else None

        def out_at(g, lag):
            if g == NH - 1 + lag - HASTE:
                return NB - 1
            b, k = divmod(g - (H1 - 1) - lag, H1)
            return b if k == 0 and 0 <= b < NB - 1 else None

        @block.sync
        def _(sp):
            sp.wait_ge(consts, 5)
            for n in range(BUFS):
                sp.dma_start(k4[4:P:32, n, :].bitcast(F32), neg_rows[:, :]).then_inc(fixed, 16)
                sp.dma_start(q4[4:P:32, n, :].bitcast(F32), zero_rows[:, :]).then_inc(fixed, 16)
            sp.wait_ge(fixed, 32 * BUFS)
            for g in range(FIRST, LAST):
                if maxima_at(g) is not None:
                    b = maxima_at(g)
                    sp.wait_ge(mT_ready, b + 1)
                    sp.dma_start(q4[4:P:32, b % BUFS, :].bitcast(F32), mT[:, :].bitcast(F32)).then_inc(m_rows, 16)
                b, k = prep_at(g, 3)
                if k in ("q", "k"):
                    t = "qk".index(k)
                    dst, parts = ((q4, (c_h, c_h, c_l, c_l)), (k4, (c_h, c_l, c_h, c_l)))[t]
                    if b >= BUFS:
                        sp.wait_ge(st_ready, (b - BUFS + 1) * H1)
                        if t == 0:
                            sp.dma_start(q4[4:P:32, b % BUFS, :].bitcast(F32), zero_rows[:, :]).then_inc(stacked, 16)
                    sp.wait_ge(cl_ready, 2 * b + t + 1)
                    for c in range(4):
                        sp.dma_start(dst[c:P:8, b % BUFS, :].bitcast(F32), parts[c][:, t, :].bitcast(F32)).then_inc(stacked, 16)

        def stacked_by(b):
            return 16 * (8 * (b + 1) + max(0, b + 1 - BUFS))

        @block.gpsimd
        def _(pool):
            pool.memset(neg_half[:, :], -0.5)
            pool.memset(zero_rows[:, :], 0.0).then_inc(consts, 1)
            pool.memset(neg_rows[:, :], -1.0).then_inc(consts, 1)
            pool.memset(k4[:, :, :].bitcast(F32), 0.0).then_inc(consts, 1)
            pool.memset(V1[:, :, :, :, :], 0.0).then_inc(ones_step, 1)
            pool.wait_ge(ones_step, 1)
            pool.memset(V1[:, :, :, :, 8:9], 1.0).then_inc(consts, 1)
            for g in range(FIRST, LAST):
                if head_at(g) is not None:
                    pool.wait_ge(e_ready, g + 1)
                    v = PT[:, g % 8, :].rearrange("p (a c n) -> p a c n", a=3, c=1)[:, 0:3:2, 0, :]
                    pool.affine_select(out=v, in_=v, compare_op=ALU.is_ge, fill=0.0, base=0,
                                       pattern=[[0, 2], [1, P]], channel_multiplier=-1).then_inc(p_ready, 1)
                b, k = prep_at(g, 1)
                if k in ("q", "k"):
                    t = "qk".index(k)
                    pool.wait_ge(ra_ready, 2 * b + t + 1)
                    pool.wait_ge(rb_ready, 2 * b + t + 1)
                    pool.tensor_tensor(rq[:, t, :], ra[:, t, :], rb[:, t, :], ALU.add).then_inc(rq_ready, 1)
                b, k = prep_at(g, 3)
                if k in ("q", "k"):
                    t = "qk".index(k)
                    pool.wait_ge(ch_ready, 2 * b + t + 1)
                    pool.tensor_tensor(c_l[:, t, :], rq[:, t, :], c_h[:, t, :].bitcast(F32), ALU.subtract).then_inc(cl_ready, 1)
                if out_at(g, OUT + 2) is not None:
                    b = out_at(g, OUT + 2)
                    pool.wait_ge(var_ready, b + 1)
                    pool.tensor_tensor(rstd[:, :], var[:, :], neg_half[:, :], ALU.pow).then_inc(rstd_ready, 1)

        @block.scalar
        def _(act):
            for g in range(FIRST, LAST):
                b, k = prep_at(g, 1)
                if k == "x":
                    act.wait_ge(xt_ready, b + 1)
                    if b >= 2:
                        act.wait_ge(pj_ready, 3 * (b - 1))
                    act.activation(xh[:, b % 2, :], TR[:, 0:L], ACT.Copy).then_inc(xh_ready, 1)
                if k == "v":
                    act.wait_ge(pj_ready, 3 * b + 3)
                    act.wait_ge(consts, 5)
                    act.activation(V1[:, b % 4, :, :, 0:D1], PJ[:, 0:L].rearrange("p (t h d) -> p t h d", t=2, d=D1), ACT.Copy).then_inc(pj_read, 1)
                b, k = prep_at(g, 2)
                if k == "x":
                    act.wait_ge(xl_ready, b + 1)
                    act.activation(xT[:, b % 2, :], TR[:, 0:L], ACT.Copy).then_inc(xT_ready, 1)
                if k in ("q", "k"):
                    t = "qk".index(k)
                    act.wait_ge(rq_ready, 2 * b + t + 1)
                    if b >= 1:
                        act.wait_ge(stacked, stacked_by(b - 1))
                    act.activation(c_h[:, t, :], rq[:, t, :], ACT.Copy).then_inc(ch_ready, 1)
                if maxima_at(g, MAX + 1) is not None:
                    b = maxima_at(g, MAX + 1)
                    act.wait_ge(mt_ready, b + 1)
                    if b >= 1:
                        act.wait_ge(m_rows, 16 * b)
                    act.activation(mT[:, :], TR[0:32, 0:L], ACT.Copy).then_inc(mT_ready, 1)
                if head_at(g) is not None:
                    act.wait_ge(st_ready, g + 1)
                    if g >= 8:
                        act.wait_ge(y_ready, (g - 8) // 4 + 1)
                    act.activation(PT[:, g % 8, :], ST[g % 2][:, 0:SW], ACT.Exp, scale=D1 ** -0.5).then_inc(e_ready, 1)
                if quad_at(g, AV + 1) is not None:
                    q = quad_at(g, AV + 1)
                    act.wait_ge(y_ready, q + 1)
                    if q >= 2:
                        act.wait_ge(yt_ready, q - 1)
                    act.activation(Yq[:, q % 2, :], YP[:, 0:L], ACT.Copy).then_inc(yq_ready, 1)
                if out_at(g, ZT + 1) is not None:
                    b = out_at(g, ZT + 1)
                    act.wait_ge(z_ready, b + 1)
                    act.activation(yT[:, :], TR[:, 0:L], ACT.Copy).then_inc(yT_ready, 1)

        @block.vector
        def _(dve):
            dve.memset(q4[:, :, :].bitcast(F32), 0.0).then_inc(consts, 1)
            for g in range(FIRST, LAST):
                b, k = prep_at(g, 1)
                if k == "x":
                    dve.wait_ge(xh_ready, b + 1)
                    dve.tensor_tensor(xl[:, b % 2, :], TR[:, 0:L], xh[:, b % 2, :].bitcast(F32), ALU.subtract).then_inc(xl_ready, 1)
                if k in ("q", "k"):
                    t = "qk".index(k)
                    dve.wait_ge(pj_ready, 3 * b + t + 1)
                    if b >= 1:
                        dve.wait_ge(rq_ready, 2 * (b - 1) + t + 1)
                    dve.tensor_tensor(ra[:, t, :], PJ[:, 0:L], mem["rope"][:, 0, :], ALU.mult).then_inc(ra_ready, 1)
                    dve.tensor_tensor(rb[:, t, :], PJ[:, L:2 * L], mem["rope"][:, 1, :], ALU.mult).then_inc(rb_ready, 1)
                h = scores_at(g)
                if h is not None:
                    b = h // H1
                    dve.wait_ge(s_ready, h + 1)
                    if b >= 2 and h % H1 == 0:
                        dve.wait_ge(mm_ready, 2 * (b - 1))
                    dve.tensor_reduce(m3[:, b % 2, h % H1, :], S[h % 2][:, 0:SW].rearrange("p (a n) -> p a n", a=3), AX.X, ALU.max).then_inc(max_done, 1)
                if maxima_at(g, MAX - 2) is not None:
                    b = maxima_at(g, MAX - 2)
                    dve.wait_ge(max_done, (b + 1) * H1)
                    dve.tensor_tensor(mm[:, 1, :], m3[:, b % 2, :, 0], m3[:, b % 2, :, 1], ALU.max).then_inc(mm_ready, 1)
                    dve.tensor_copy(mm[:, 0, :], m3[:, b % 2, :, 2]).then_inc(mm_ready, 1)
                    dve.wait_ge(mm_ready, 2 * b + 2)
                    if b >= 1:
                        dve.wait_ge(mt_ready, b)
                    by_pair = mm[:, :, :].rearrange("p t (j r) -> p t r j", r=2)
                    for t in range(2):
                        i = dve.tensor_copy(mx[:, t, :, 0, :], by_pair[:, t])
                    i.then_inc(mxh_ready, 1)
                    dve.wait_ge(mxh_ready, b + 1)
                    for t in range(2):
                        i = dve.tensor_tensor(mx[:, t, :, 1, :], by_pair[:, t], mx[:, t, :, 0, :].bitcast(F32), ALU.subtract)
                    i.then_inc(mx_ready, 1)
                q = quad_at(g, TQ + 1)
                if q is not None:
                    b, qq = divmod(q, 4)
                    dve.wait_ge(yt_ready, q + 1)
                    yt = MI[:, 0:L].rearrange("p (t i c) -> p t i c", t=2, i=4)
                    dve.reciprocal(rden[:, :, :], yt[:, :, :, D1]).then_inc(den_ready, 1)
                    dve.wait_ge(den_ready, q + 1)
                    if b >= 2 and qq == 0:
                        dve.wait_ge(z_ready, b - 1)
                    for t in range(2):
                        i = dve.tensor_tensor(yn[:, b % 2, t, qq * 32:qq * 32 + 32].rearrange("p (i d) -> p i d", i=4),
                                              yt[:, t, :, 0:D1], rden[:, t, :, None].to_broadcast([P, 4, D1]), ALU.mult)
                    i.then_inc(yn_ready, 1)
                b = out_at(g, OUT + 1)
                if b is not None:
                    dve.wait_ge(o_ready, b + 1)
                    dve.tensor_tensor(res[:, b % 2, :, :], PJ[:, 0:2 * D].rearrange("p (t d) -> p t d", t=2), X[:, 2 * b:2 * b + 2, :], ALU.add).then_inc(res_ready, 1)
                    dve.wait_ge(res_ready, b + 1)
                    norm_stats(dve, res[:, b % 2], stats, mv[:, b % 2], var, 2, ln_step, 2 * b, var_ready)
                b = out_at(g, OUT + 3)
                if b is not None:
                    dve.wait_ge(rstd_ready, b + 1)
                    norm_apply(dve, X[:, 2 * b:2 * b + 2, :], res[:, b % 2], mv[:, b % 2], rstd, 2).then_inc(x_done, 1)

        def use_order():
            tr, pj = [], []
            for g in range(FIRST, LAST):
                b, k = prep_at(g)
                if k == "x":
                    tr.append(("x", b))
                elif k:
                    pj.append((k, b))
                if maxima_at(g) is not None:
                    tr.append(("m", maxima_at(g)))
                if out_at(g, ZT) is not None:
                    tr.append(("z", out_at(g, ZT)))
                if out_at(g, OUT) is not None:
                    pj.append(("o", out_at(g, OUT)))
            return tr, pj

        TR_USES, PJ_USES = use_order()

        @block.tensor
        def _(pe):
            def bank_free(uses, use):
                at = uses.index(use)
                if at == 0:
                    return
                k, b = uses[at - 1]
                if k == "x":
                    pe.wait_ge(xT_ready, b + 1)
                elif k == "m":
                    pe.wait_ge(mT_ready, b + 1)
                elif k == "z":
                    pe.wait_ge(yT_ready, b + 1)
                elif k in "qk":
                    pe.wait_ge(ra_ready, 2 * b + "qk".index(k) + 1)
                    pe.wait_ge(rb_ready, 2 * b + "qk".index(k) + 1)
                elif k == "v":
                    pe.wait_ge(pj_read, b + 1)
                else:
                    pe.wait_ge(res_ready, b + 1)

            for g in range(FIRST, LAST):
                b, k = prep_at(g)
                if k:
                    p = b % 2
                    if k == "x":
                        bank_free(TR_USES, ("x", b))
                        for t in range(2):
                            i = pe.transpose(TR[:, t * P:(t + 1) * P], X[:, 2 * b + t, :], ident[:, :])
                        i.then_inc(xt_ready, 1)
                    else:
                        bank_free(PJ_USES, (k, b))
                        if k == "v":
                            for t in range(2):
                                i = pe.matmul(PJ[:, t * P:(t + 1) * P], xT[:, p, t * P:(t + 1) * P], mem["a1_wv"][:, :], start=True, stop=True)
                        else:
                            pe.wait_ge(xT_ready, b + 1)
                            pe.wait_ge(xl_ready, b + 1)
                            w = 2 * "qk".index(k)
                            for s in range(2):
                                i = three_pass(pe, PJ[:, s * L:(s + 1) * L], mem["a1_wqk_h"][:, (w + s) * P:(w + s + 1) * P],
                                               mem["a1_wqk_l"][:, (w + s) * P:(w + s + 1) * P], xh[:, p, :], xl[:, p, :])
                        i.then_inc(pj_ready, 1)
                h = scores_at(g)
                if h is not None:
                    b, hh = divmod(h, H1)
                    j, par = divmod(hh, 2)
                    if hh == 0:
                        pe.wait_ge(stacked, stacked_by(b))
                        pe.wait_ge(fixed, 32 * BUFS)
                    if h >= 2:
                        pe.wait_ge(max_done, h - 1)
                    rows = slice(64 * par, 64 * par + 64)
                    qq, kk = q4[rows, b % BUFS, j * L:(j + 1) * L], k4[rows, b % BUFS, j * L:(j + 1) * L]
                    pe.matmul(S[h % 2][:, 0:L], qq[:, P:L], kk[:, 0:L], start=True, stop=False, skip_group_check=True)
                    pe.matmul(S[h % 2][:, L:SW], qq[:, 0:P], kk[:, 0:P], start=False, stop=False, skip_group_check=True)
                    pe.matmul(S[h % 2][:, P:SW], mem["ident_b"][:, :], mem["mask_b"][:, :], start=False, stop=True, skip_group_check=True).then_inc(s_ready, 1)
                if maxima_at(g) is not None:
                    b = maxima_at(g)
                    bank_free(TR_USES, ("m", b))
                    pe.wait_ge(mx_ready, b + 1)
                    for t in range(2):
                        i = pe.transpose(TR[0:32, t * P:(t + 1) * P], mx[:, t, :, :, :].rearrange("p r c j -> p (r c j)").bitcast(F32), ident[:, :])
                    i.then_inc(mt_ready, 1)
                if head_at(g) is not None:
                    b, hh = divmod(g, H1)
                    j, par = divmod(hh, 2)
                    if hh == 0:
                        pe.wait_ge(m_rows, 16 * (b + 1))
                    if g >= 2:
                        pe.wait_ge(e_ready, g - 1)
                    rows = slice(64 * par, 64 * par + 64)
                    qq, kk = q4[rows, b % BUFS, j * L:(j + 1) * L], k4[rows, b % BUFS, j * L:(j + 1) * L]
                    pe.matmul(ST[g % 2][:, 0:L], kk[:, 0:P], qq[:, 0:L], start=True, stop=True)
                    pe.matmul(ST[g % 2][:, L:SW], kk[:, P:L], qq[:, P:L], start=True, stop=True).then_inc(st_ready, 1)
                q = quad_at(g, AV)
                if q is not None:
                    b = q // 4
                    pe.wait_ge(p_ready, 4 * q + 4)
                    pe.wait_ge(pj_read, b + 1)
                    if q >= 1:
                        pe.wait_ge(yq_ready, q)
                    for t in range(2):
                        for i4 in range(4):
                            hg = 4 * q + i4
                            cols = slice(0, L) if t == 0 else slice(L, SW)
                            i = pe.matmul(YP[32 * i4:32 * i4 + 32, t * P:L], V1[:, b % 4, t, hg % H1, :], PT[:, hg % 8, cols],
                                          start=(t == 0), stop=(t == 1), skip_group_check=True)
                    i.then_inc(y_ready, 1)
                q = quad_at(g, TQ)
                if q is not None:
                    pe.wait_ge(yq_ready, q + 1)
                    if q >= 1:
                        pe.wait_ge(yn_ready, q)
                    for t in range(2):
                        i = pe.transpose(MI[:, t * P:(t + 1) * P], Yq[:, q % 2, t * P:(t + 1) * P], ident[:, :])
                    i.then_inc(yt_ready, 1)
                b = out_at(g, ZT)
                if b is not None:
                    bank_free(TR_USES, ("z", b))
                    pe.wait_ge(yn_ready, 4 * (b + 1))
                    for t in range(2):
                        i = pe.transpose(TR[:, t * P:(t + 1) * P], yn[:, b % 2, t, :], ident[:, :])
                    i.then_inc(z_ready, 1)
                b = out_at(g, OUT)
                if b is not None:
                    bank_free(PJ_USES, ("o", b))
                    pe.wait_ge(yT_ready, b + 1)
                    for t in range(2):
                        i = pe.matmul(PJ[:, t * D:(t + 1) * D], yT[:, t * P:(t + 1) * P], mem["a1_wo"][:, :], start=True, stop=True)
                    i.then_inc(o_ready, 1)


def experts1(nc, mem, dr, out):
    X, ident = mem["X"], mem["ident"]
    TB = BT // P
    NS = NBLK * NE1
    ctx = ExitStack()
    with ctx:
        sb = lambda n, s, d=F32: ctx.enter_context(nc.sbuf_tensor("f1_" + n, s, d))
        sem = lambda n: ctx.enter_context(nc.semaphore("f1_" + n))
        w_h, w_l, w3 = mem["f1_w_h"], mem["f1_w_l"], mem["f1_w3"]
        xT = sb("xT", [P, 2, TB, P])
        xh = sb("xh", [P, 2, BT], F32R)
        xl = sb("xl", [P, 2, BT], F32R)
        sc = sb("sc", [P, NT, NE1])
        top = sb("top", [P, NT, 8])
        idx = sb("idx", [P, NT, 8], U32)
        idf = sb("idf", [P, NT, 2])
        dlt = sb("dlt", [P, NT])
        ex = sb("ex", [P, NT])
        prob = sb("prob", [P, 2, NT])
        den = sb("den", [P, NT])
        oh = sb("oh", [P, 2, NT, NE1])
        gate = sb("gate", [P, NT, NE1])
        e_base = sb("e_base", [P, NT])
        sg = sb("sg", [P, 4, BT])
        hid = sb("hid", [P, 2, FC1, BT])
        acc = sb("acc", [P, 2, TB, D])
        fin = sb("fin", [P, 2, TB, D])
        stats = sb("stats", [P, TB, 6])
        mv = sb("mv", [P, 2, TB, 2])
        var = sb("var", [P, TB])
        rstd = sb("rstd", [P, TB])
        neg_half = sb("neghalf", [P, TB])
        T = ctx.enter_context(nc.psum_tensor("f1_T", [P, 512], F32))
        G = ctx.enter_context(nc.psum_tensor("f1_G", [P, 512], F32))
        H = [[ctx.enter_context(nc.psum_tensor(f"f1_H{i}{k}", [P, 512], F32)) for k in range(2)] for i in range(2)]
        O = [ctx.enter_context(nc.psum_tensor(f"f1_O{i}", [P, 512], F32)) for i in range(2)]
        t_ready, xT_ready, xh_ready, xl_ready = sem("t_ready"), sem("xT_ready"), sem("xh_ready"), sem("xl_ready")
        g_ready, sc_ready, top_ready, idx_ready, g_step, gate_ready = (sem(n) for n in "g_ready sc_ready top_ready idx_ready g_step gate_ready".split())
        dlt_ready, ex_ready = sem("dlt_ready"), sem("ex_ready")
        h1_ready, h2_ready = sem("h1_ready"), sem("h2_ready")
        silu_done, hid_done = sem("silu_done"), sem("hid_done")
        o_ready, acc_done = sem("o_ready"), sem("acc_done")
        ln_step, var_ready, rstd_ready, fin_ready, consts = (sem(n) for n in "ln_step var_ready rstd_ready fin_ready consts".split())
        stored = [sem("stored0"), sem("stored1")]
        block = ctx.enter_context(nc.Block())

        @block.sync
        def _(sp):
            for i in range(NBLK):
                sp.wait_ge(fin_ready, i + 1)
                sp.dma_start(out[:, TB * i:TB * i + TB, :], fin[:, i % 2, :, :]).then_inc(stored[i % 2], 16)
            for p in range(2):
                sp.wait_ge(stored[p], 16 * NBLK // 2)

        @block.gpsimd
        def _(pool):
            pool.memset(neg_half[:, :], -0.5).then_inc(consts, 1)
            pool.memset(e_base[:, :], float(np.e)).then_inc(consts, 1)
            pool.wait_ge(dlt_ready, 1)
            pool.wait_ge(consts, 2)
            pool.tensor_tensor(ex[:, :], e_base[:, :], dlt[:, :], ALU.pow).then_inc(ex_ready, 1)
            for i in range(NBLK):
                pool.wait_ge(var_ready, i + 1)
                pool.tensor_tensor(rstd[:, :], var[:, :], neg_half[:, :], ALU.pow).then_inc(rstd_ready, 1)

        def prepare_at(n, c):
            i, e = divmod(n, NE1)
            return i + 1 if c == 0 and e == 4 and i + 1 < NBLK else None

        @block.scalar
        def _(act):
            def prepare(i, gates):
                act.wait_ge(t_ready, i + 1 if gates is None else gates)
                if gates is not None:
                    k = gates - 1
                    if k >= 2:
                        act.wait_ge(g_ready, k - 1)
                    act.activation(xT[:, k % 2, :, :], T[:, :].rearrange("p (t n) -> p t n", t=TB), ACT.Copy).then_inc(xT_ready, 1)

            def split(i, count):
                act.wait_ge(t_ready, count)
                if i >= 2:
                    act.wait_ge(h2_ready, (i - 1) * NE1 * FC1)
                act.activation(xh[:, i % 2, :], T[:, :], ACT.Copy).then_inc(xh_ready, 1)

            for i in range(NBLK):
                prepare(i, i + 1)
            split(0, NBLK + 1)
            for n in range(NS):
                for c in range(FC1):
                    m = n * FC1 + c
                    act.wait_ge(h1_ready, m + 1)
                    if m >= 4:
                        act.wait_ge(hid_done, m - 3)
                    act.activation(sg[:, m % 4, :], H[m % 2][0][:, :], ACT.Silu).then_inc(silu_done, 1)
                    i = prepare_at(n, c)
                    if i is not None:
                        split(i, NBLK + 1 + i)

        @block.vector
        def _(dve):
            def split(i):
                dve.wait_ge(xh_ready, i + 1)
                dve.tensor_tensor(xl[:, i % 2, :], T[:, :], xh[:, i % 2, :].bitcast(F32), ALU.subtract).then_inc(xl_ready, 1)

            def route():
                def chain(ins, count):
                    ins.then_inc(g_step, 1)
                    dve.wait_ge(g_step, count)
                for t in range(NT):
                    k = dve.max(top[:, t, :], sc[:, t, :])
                k.then_inc(top_ready, 1)
                dve.wait_ge(top_ready, 1)
                dve.tensor_tensor(dlt[:, :], top[:, :, 1], top[:, :, 0], ALU.subtract).then_inc(dlt_ready, 1)
                for t in range(NT):
                    k = dve.max_index(idx[:, t, :], top[:, t, :], sc[:, t, :])
                k.then_inc(idx_ready, 1)
                dve.wait_ge(idx_ready, 1)
                chain(dve.tensor_copy(idf[:, :, :], idx[:, :, 0:2]), 1)
                for k in range(2):
                    chain(dve.tensor_tensor(oh[:, k, :, :], mem["iota8"][:, None, :].to_broadcast([P, NT, NE1]),
                                            idf[:, :, k:k + 1].to_broadcast([P, NT, NE1]), ALU.is_equal), 2 + k)
                dve.wait_ge(ex_ready, 1)
                chain(dve.tensor_scalar(den[:, :], ex[:, :], 1.0, None, ALU.add), 4)
                chain(dve.reciprocal(prob[:, 0, :], den[:, :]), 5)
                chain(dve.tensor_tensor(prob[:, 1, :], prob[:, 0, :], ex[:, :], ALU.mult), 6)
                for k in range(2):
                    chain(dve.tensor_tensor(oh[:, k, :, :], oh[:, k, :, :], prob[:, k, :, None].to_broadcast([P, NT, NE1]), ALU.mult), 7 + k)
                dve.tensor_tensor(gate[:, :, :], oh[:, 0, :, :], oh[:, 1, :, :], ALU.add).then_inc(gate_ready, 1)
                dve.wait_ge(gate_ready, 1)

            def combine(n):
                i, e = divmod(n, NE1)
                dve.wait_ge(o_ready, n + 1)
                if e > 0:
                    dve.wait_ge(acc_done, n)
                for t in range(TB):
                    prior = X[:, TB * i + t, :] if e == 0 else acc[:, i % 2, t, :]
                    k = dve.scalar_tensor_tensor(acc[:, i % 2, t, :], O[n % 2][:, t * D:(t + 1) * D], gate[:, TB * i + t, e:e + 1],
                                                 prior, ALU.mult, ALU.add)
                k.then_inc(acc_done, 1)

            def finish(i):
                dve.wait_ge(acc_done, (i + 1) * NE1)
                norm_stats(dve, acc[:, i % 2], stats, mv[:, i % 2], var, TB, ln_step, 2 * i, var_ready)

            def finish2(i):
                dve.wait_ge(rstd_ready, i + 1)
                if i >= 2:
                    dve.wait_ge(stored[i % 2], 16 * (i // 2))
                norm_apply(dve, fin[:, i % 2], acc[:, i % 2], mv[:, i % 2], rstd, TB).then_inc(fin_ready, 1)

            for i in range(NBLK):
                dve.wait_ge(g_ready, i + 1)
                dve.tensor_copy(sc[:, TB * i:TB * i + TB, :], G[:, i * TB * NE1:(i + 1) * TB * NE1].rearrange("p (t e) -> p t e", e=NE1)).then_inc(sc_ready, 1)
            split(0)
            dve.wait_ge(sc_ready, NBLK)
            route()
            for n in range(NS + 2):
                for c in range(FC1):
                    m = n * FC1 + c
                    if n < NS:
                        dve.wait_ge(silu_done, m + 1)
                        dve.wait_ge(h2_ready, m + 1)
                        if n >= 2 and c == 0:
                            dve.wait_ge(o_ready, n - 1)
                        dve.tensor_tensor(hid[:, n % 2, c, :], H[m % 2][1][:, :], sg[:, m % 4, :], ALU.mult).then_inc(hid_done, 1)
                        i = prepare_at(n, c)
                        if i is not None:
                            split(i)
                if n >= 2:
                    combine(n - 2)
                    if (n - 2) % NE1 == NE1 - 1:
                        finish((n - 2) // NE1)
                if n >= 3 and (n - 3) % NE1 == NE1 - 1:
                    finish2((n - 3) // NE1)
            finish2(NBLK - 1)

        @block.tensor
        def _(pe):
            def transpose_x(i, use):
                if use >= 1:
                    if use <= NBLK:
                        pe.wait_ge(xT_ready, use)
                    else:
                        pe.wait_ge(xl_ready, use - NBLK)
                for t in range(TB):
                    k = pe.transpose(T[:, t * P:(t + 1) * P], X[:, TB * i + t, :], ident[:, :])
                k.then_inc(t_ready, 1)

            for i in range(NBLK):
                transpose_x(i, i)
                pe.wait_ge(xT_ready, i + 1)
                if i >= 1:
                    pe.wait_ge(sc_ready, i)
                for t in range(TB):
                    col = (i * TB + t) * NE1
                    k = pe.matmul(G[:, col:col + NE1], xT[:, i % 2, t, :], mem["f1_wg"][:, :], start=True, stop=True)
                k.then_inc(g_ready, 1)
            transpose_x(0, NBLK)
            for n in range(NS + 1):
                i, e = divmod(n, NE1)
                for c in range(FC1):
                    m = n * FC1 + c
                    if n < NS:
                        if e == 0 and c == 0:
                            pe.wait_ge(xl_ready, i + 1)
                        if m >= 2:
                            pe.wait_ge(hid_done, m - 1)
                        for w, done in enumerate((h1_ready, h2_ready)):
                            col = (2 * e + w) * F1 + c * P
                            three_pass(pe, H[m % 2][w][:, :], w_h[:, col:col + P], w_l[:, col:col + P], xh[:, i % 2, :], xl[:, i % 2, :]).then_inc(done, 1)
                        k = prepare_at(n, c)
                        if k is not None:
                            transpose_x(k, NBLK + k)
                    if n >= 1:
                        r = n - 1
                        if c == 0:
                            pe.wait_ge(hid_done, n * FC1)
                            if r >= 2:
                                pe.wait_ge(acc_done, r - 1)
                        for t in (2 * c, 2 * c + 1):
                            for f in range(FC1):
                                k = pe.matmul(O[r % 2][:, t * D:(t + 1) * D], hid[:, r % 2, f, t * P:(t + 1) * P],
                                              w3[:, (r % NE1) * FC1 + f, :], start=(f == 0), stop=(f == FC1 - 1))
                if n >= 1:
                    k.then_inc(o_ready, 1)


def program(nc, dr, out, stop=4):
    ctx = ExitStack()
    with ctx:
        sb = lambda n, s, d=F32: ctx.enter_context(nc.sbuf_tensor(n, s, d))
        sem = lambda n: ctx.enter_context(nc.semaphore(n))
        mem = dict(X=sb("X", [P, NT, D]), RES=sb("RES", [P, 2, 2, D]), ident=sb("ident", [P, P]),
                   w1=sb("w1", [P, NE0, HID]), w1_h=sb("w1_h", [P, NE0, HID], F32R), w1_l=sb("w1_l", [P, NE0, HID], F32R),
                   w2=sb("w2", [P, NE0 * HC, D]), b1=sb("b1", [P, NE0 * HC]), b2=sb("b2", [P, NE0, D]),
                   gate_w=sb("gate_w", [P, 2]), w_split=sem("w_split"))
        in_w1, in_f0, later, out_done = sem("in_w1"), sem("in_f0"), sem("later"), sem("out_done")
        mem["in_w1"] = in_w1

        def load_later(sp):
            dma_in(sp, mem["w1"][:, :, :], dr["f0_w1"], in_w1)
            for name in ("w2", "b1", "b2", "gate_w"):
                dma_in(sp, mem[name][(slice(None),) * len(mem[name].shape)], dr["f0_" + name], in_f0)
            dma_in(sp, mem["ident"][:, :], dr["ident"], in_f0)

        def wait_later(sp):
            sp.wait_ge(in_f0, 80)

        mem["load_later"], mem["wait_later"] = load_later, wait_later
        attention0(nc, mem, dr)
        ctx2 = ExitStack()
        with ctx2:
            sb = lambda n, s, d=F32: ctx2.enter_context(nc.sbuf_tensor(n, s, d))
            WC = 2 * NE1 * F1
            mem |= dict(f1_w=sb("f1_w", [P, WC]), f1_w_h=sb("f1_w_h", [P, WC], F32R), f1_w_l=sb("f1_w_l", [P, WC], F32R),
                        f1_w3=sb("f1_w3", [P, NE1 * FC1, D]), f1_wg=sb("f1_wg", [P, NE1]), iota8=sb("iota8", [P, NE1]),
                        a1_wqk=sb("a1_wqk", [P, 4 * P]), a1_wqk_h=sb("a1_wqk_h", [P, 4 * P], F32R), a1_wqk_l=sb("a1_wqk_l", [P, 4 * P], F32R),
                        a1_wv=sb("a1_wv", [P, P]), a1_wo=sb("a1_wo", [P, P]), rope=sb("rope", [P, 2, L]),
                        ident_b=sb("ident_b", [P, P], BF16), mask_b=sb("mask_b", [P, L], BF16))
            in_q, in_f1, in_l1 = sem("in_q"), sem("in_f1"), sem("in_l1")

            def load_layer1(sp):
                dma_in(sp, mem["a1_wqk"][:, :], dr["a1_wqk"], in_q)
                dma_in(sp, mem["f1_w"][:, :], dr["f1_w"], in_f1)
                names = ("f1_w3", "f1_wg", "iota8", "a1_wv", "a1_wo", "rope", "ident_b", "mask_b")
                for name in names:
                    dma_in(sp, mem[name][(slice(None),) * len(mem[name].shape)], dr[name], in_l1)
                sp.wait_ge(in_l1, 16 * len(names))

            mem["load_layer1"] = load_layer1
            half = lambda n, k: mem[n][:, k * WC // 2:(k + 1) * WC // 2]
            mem["splits"] = [[], [(mem["a1_wqk"][:, :], mem["a1_wqk_h"][:, :], mem["a1_wqk_l"][:, :], in_q, 4 * P)]] + [
                [(half("f1_w", k), half("f1_w_h", k), half("f1_w_l", k), in_f1, WC // 2)] for k in range(2)]
            feed_forward0(nc, mem, dr)
            if stop >= 3:
                attention1(nc, mem, dr)
            if stop >= 4:
                experts1(nc, mem, dr, out)
            else:
                with nc.Block() as block:
                    @block.sync
                    def _(sp):
                        sp.dma_start(out, mem["X"][:, :, :]).then_inc(out_done, 16)
                        sp.wait_ge(out_done, 16)


def layouts(i):
    f = lambda a: np.ascontiguousarray(a)
    x = np.asarray(i["L0_attn_hidden_states"]).reshape(N, D)
    a = {"xT": f(x.T), "x": f(x.reshape(NT, P, D).transpose(1, 0, 2))}
    heads = [[2 * (2 * aa + g) + par for par in range(2) for _ in range(FD) for aa in range(4)] for g in range(2)]
    feats = [ff for _ in range(2) for ff in range(FD) for _ in range(4)]
    cols = [np.array(heads[g]) * FD + np.array(feats) for g in range(2)]
    a["a0_wqk"] = f(np.stack([np.asarray(i[w]).T[:, cols[g]] for w in ("L0_attn_Wq", "L0_attn_Wk") for g in range(2)], 1))
    a["a0_wv"] = f(np.asarray(i["L0_attn_Wv"]).T)
    a["a0_wo"] = f(np.asarray(i["L0_attn_Wo"]).T.reshape(NPAIR, P, D).transpose(1, 0, 2))
    a["a0_g"] = f(np.tile(np.asarray(i["L0_attn_g_weight"]), 2).reshape(P, 1))
    m, n = np.arange(P)[:, None], np.arange(P)[None, :]
    tri = (m <= n).astype(np.float32)
    a["mask0"] = f(np.concatenate([tri, np.ones((P, P), np.float32), tri], 1))
    ss, es = np.zeros((P, NPAIR, 32), np.float32), np.zeros((P, NPAIR, P), np.float32)
    for j in range(NPAIR):
        for par in range(2):
            ss[64 * par:64 * par + 64, j, 2 * (j // 4) + par] = 1
            es[32 * (j % 4) + 2 * (j // 4) + par, j, 64 * par:64 * par + 64] = 1
    a["sum_sel"], a["exp_sel"] = ss, es
    a["ident"] = np.eye(P, dtype=np.float32)
    g = lambda n: np.asarray(i["L0_ffn_" + n])
    a["f0_w1"] = f(np.stack([g("w1")[0], g("w1")[1], g("sw1")], 1))
    a["f0_w2"] = f(np.concatenate([g("w2")[0], g("w2")[1], g("sw2")], 0).reshape(NE0 * HC, P, D).transpose(1, 0, 2))
    a["f0_b1"] = f(np.concatenate([g("b1")[0], g("b1")[1], g("sb1")]).reshape(NE0 * HC, P).T)
    a["f0_b2"] = f(np.broadcast_to(np.stack([g("b2")[0], g("b2")[1], g("sb2")])[None], (P, NE0, D)))
    a["f0_gate_w"] = f(g("gate_w").T)
    wqkv = np.asarray(i["L1_attn_W_qkv"])
    col = np.array([(2 * j + par) * D1 + d for par in range(2) for d in range(D1) for j in range(NPAIR)])
    swap = col // D1 * D1 + (col % D1 + D1 // 2) % D1
    a["a1_wqk"] = f(np.concatenate([wqkv[:, part * D + c] for part in range(2) for c in (col, swap)], 1))
    a["a1_wv"] = f(wqkv[:, 2 * D:])
    a["a1_wo"] = f(np.asarray(i["L1_attn_W_o"]))
    freqs = np.arange(D1 // 2, dtype=np.float32) / np.float32(D1 // 2)
    theta = np.float32(1.0) / np.float32(10000.0) ** freqs
    ang = np.arange(L, dtype=np.float32)[None, :] * theta[(col % D1) % (D1 // 2)][:, None]
    sign = np.where(col % D1 < D1 // 2, -1.0, 1.0).astype(np.float32)[:, None]
    a["rope"] = f(np.stack([np.cos(ang), sign * np.sin(ang)], 1).astype(np.float32))
    bf16 = mybir.dt.np(BF16)
    a["ident_b"] = np.eye(P).astype(bf16)
    a["mask_b"] = f(np.tile(np.where(n > m, -3e38, 0.0), (1, 2)).astype(bf16))
    h = lambda n: np.asarray(i["L1_ffn_" + n])
    a["f1_w"] = f(np.stack([h("W1"), h("W2")], 1).reshape(2 * NE1 * F1, D).T)
    a["f1_w3"] = f(h("W3").transpose(0, 2, 1).reshape(NE1 * FC1, P, D).transpose(1, 0, 2))
    a["f1_wg"] = f(h("Wg").T)
    a["iota8"] = f(np.broadcast_to(np.arange(NE1, dtype=np.float32), (P, NE1)))
    return a


def kernel(**inputs):
    import concourse.bacc as bacc
    from concourse.bass_utils import run_bass_kernel_spmd

    arrays = layouts(inputs)
    nc = bacc.Bacc("TRN2", target_bir_lowering=False, num_devices=1)
    dr = {n: nc.dram_tensor("in_" + n, a.shape, mybir.dt.from_np(a.dtype), kind="ExternalInput").ap() for n, a in arrays.items()}
    out = nc.dram_tensor("out", (N, D), F32, kind="ExternalOutput").ap()
    program(nc, dr, out.rearrange("(t p) d -> p t d", p=P))
    r = run_bass_kernel_spmd(nc, [{"in_" + n: a for n, a in arrays.items()}], core_ids=[0])
    return r.results[0]["out"].reshape(NB, L, D)
```

```python
from contextlib import ExitStack

import numpy as np
import concourse.bass as bass
from concourse import mybir

F32 = mybir.dt.float32
F32R = mybir.dt.float32r
BF16 = mybir.dt.bfloat16
U32 = mybir.dt.uint32
ACT = mybir.ActivationFunctionType
ALU = mybir.AluOpType
AX = mybir.AxisListType

P = 128
D = 128
NB, L = 8, 256
N = NB * L
NT = N // P
LN_EPS = 1e-5
H0, FD, E0 = 16, 16, 64
NPAIR = H0 // 2
RMS_EPS = 1e-5
SW = 384
HID, NE0 = 512, 3
HC = HID // P
H1, D1 = 16, 8
NE1, F1 = 8, 256
FC1 = F1 // P
BT = 512
NBLK = N // BT
TB = BT // P


def dma_in(eng, dst, src, done):
    eng.dma_start(dst, src).then_inc(done, 16)


def three_pass(pe, out, a_hi, a_lo, b_hi, b_lo):
    pe.matmul(out, a_hi, b_hi, start=True, stop=False)
    pe.matmul(out, a_lo, b_hi, start=False, stop=False)
    return pe.matmul(out, a_hi, b_lo, start=False, stop=True)


def lagged(b, v, j, lag=2):
    if not 0 <= v * NPAIR + j - lag < NB * NPAIR:
        return None
    return (b, v, j - lag) if j >= lag else (b - 1, v - 1, j - lag + NPAIR)


def attention0(nc, mem, dr):
    X, RES, in_f0 = mem["X"], mem["RES"], mem["in_f0"]
    ctx = ExitStack()
    with ctx:
        sb = lambda n, s, d=F32: ctx.enter_context(nc.sbuf_tensor(n, s, d))
        sem = lambda n: mem["scope"].enter_context(nc.semaphore(n))
        xT = sb("a0_xT", [P, N])
        w_qk = sb("a0_wqk", [P, 4, P])
        w_v = sb("a0_wv", [P, H0 * E0])
        qk_h = sb("a0_wqk_h", [P, 4, P], F32R)
        qk_l = sb("a0_wqk_l", [P, 4, P], F32R)
        v_h = sb("a0_wv_h", [P, H0 * E0], F32R)
        v_l = sb("a0_wv_l", [P, H0 * E0], F32R)
        w_o = sb("a0_wo", [P, NPAIR, D])
        w_og = sb("a0_wog", [P, NPAIR, D])
        g_col = sb("a0_g", [P, 1])
        mask = sb("a0_mask", [P, SW])
        sum_sel = sb("a0_sumsel", [P, NPAIR, 32])
        exp_selw = sb("a0_expselw", [P, NPAIR, P])
        exp_sel = sb("a0_expsel", [P, NPAIR, P], F32R)
        neg_half = sb("a0_neghalf", [P, 2])
        one_col = sb("a0_one", [P, 1])
        warm = sb("a0_warm", [P, 1])
        xs_h = sb("a0_xs_h", [P, 2, L], F32R)
        xs_l = sb("a0_xs_l", [P, 2, L], F32R)
        c_h = sb("a0_c_h", [P, 2, 2 * L], F32R)
        c_l = sb("a0_c_l", [P, 2, 2 * L], F32R)
        q4 = sb("a0_q4", [P, 2, NPAIR * L], F32R)
        k4 = sb("a0_k4", [P, 2, NPAIR * L], F32R)
        V = sb("a0_V", [P, 2, 2, H0 * E0])
        UA = sb("a0_UA", [P, 4, 2, SW])
        Y = sb("a0_Y", [P, 2, NPAIR, L])
        Y2 = sb("a0_Y2", [P, 2, NPAIR, L])
        YN = sb("a0_YN", [P, NPAIR, L])
        ms = sb("a0_ms", [P, L])
        rms = sb("a0_rms", [P, L])
        rr = sb("a0_rr", [P, L])
        rr_h = sb("a0_rr_h", [P, L], F32R)
        rr_parts = sb("a0_rr_parts", [P, L], F32R)
        low_row = sb("a0_low_row", [P, 1])
        st = sb("a0_st", [P, 2, 6])
        mv = sb("a0_mv", [P, 2, 2])
        ve = sb("a0_ve", [P, 2])
        rs = sb("a0_rs", [P, 2])
        S = [ctx.enter_context(nc.psum_tensor(f"a0_S{i}", [P, 2, 512], F32)) for i in range(2)]
        YP = [ctx.enter_context(nc.psum_tensor(f"a0_Y{i}", [P, 512], F32)) for i in range(2)]
        PJ = ctx.enter_context(nc.psum_tensor("a0_PJ", [P, 512], F32))
        MI = ctx.enter_context(nc.psum_tensor("a0_MI", [P, 512], F32))

        in_x0, in_x1, in_x, in_wqk, in_wv, in_mask, in_c, in_res, in_g, in_o = (sem(f"a0_in_{n}") for n in "x0 x1 x wqk wv mask c res g o".split())
        w_split = sem("a0_w_split")
        consts = sem("a0_consts")
        xs_hi = sem("a0_xs_hi")
        xs_ready = sem("a0_xs_ready")
        pj_ready = sem("a0_pj_ready")
        pj_read = sem("a0_pj_read")
        hi_ready = sem("a0_hi_ready")
        lo_ready = sem("a0_lo_ready")
        stacked = sem("a0_stacked")
        s_ready = sem("a0_s_ready")
        sq_done = sem("a0_sq_done")
        a_ready = sem("a0_a_ready")
        y_ready = sem("a0_y_ready")
        y_copied = sem("a0_y_copied")
        y2_ready = sem("a0_y2_ready")
        mi_ready = sem("a0_mi_ready")
        mi_read = sem("a0_mi_read")
        rr_ready = sem("a0_rr_ready")
        rms_ready = sem("a0_rms_ready")
        rr_hi = sem("a0_rr_hi")
        rr_split = sem("a0_rr_split")
        ln_step = sem("a0_ln_step")
        ve_ready = sem("a0_ve_ready")
        rs_ready = sem("a0_rs_ready")
        x_done = sem("a0_x_done")
        w_step = sem("a0_w_step")
        warm_done = sem("a0_warm_done")

        def spread_at(b, v, j):
            if j >= 5 and 1 <= v <= NB:
                return b, v, j - 5
            return (b - 1, v - 1, 3) if j == 0 and v >= 2 else None

        def proj_bank(v, u):
            return (S[0][:, 0, :], S[0][:, 1, :], S[1][:, 0, :], S[1][:, 1, :], YP[0], YP[1], MI, PJ)[u] if v == 0 else PJ

        def spread_bank(v, g):
            return S[g // 2][:, g % 2, :] if v == NB else MI[:, :]

        MI_OF = lambda b: 5 + 6 * (b - 2)

        block = mem["block"]

        @block.sync
        def _(sp):
            dma_in(sp, w_qk[:, :, :], dr["a0_wqk"], in_wqk)
            dma_in(sp, xT[:, 0:L], dr["xT"][:, 0:L], in_x0)
            dma_in(sp, w_v[:, :], dr["a0_wv"], in_wv)
            dma_in(sp, mask[:, :], dr["mask0"], in_mask)
            dma_in(sp, xT[:, L:2 * L], dr["xT"][:, L:2 * L], in_x1)

            def stack(b, v, par):
                for t, (dst, parts) in enumerate(((q4, (c_h, c_h, c_l, c_l)), (k4, (c_h, c_l, c_h, c_l)))):
                    sp.wait_ge(lo_ready, b * 4 + 2 * t + 2)
                    if v >= 2 and t == 0:
                        sp.wait_ge(s_ready, (b - 1) * NPAIR)
                    for c in range(4):
                        sp.dma_start(dst[c:P:4, par, :].bitcast(F32), parts[c][:, t, :].bitcast(F32)).then_inc(stacked, 16)

            stack(0, 0, 0)
            dma_in(sp, sum_sel[:, :, :], dr["sum_sel"], in_c)
            dma_in(sp, exp_selw[:, :, :], dr["exp_sel"], in_c)
            dma_in(sp, xT[:, 2 * L:N], dr["xT"][:, 2 * L:N], in_x)
            dma_in(sp, w_o[:, :, :], dr["a0_wo"], in_o)
            dma_in(sp, g_col[:, :], dr["a0_g"], in_g)
            dma_in(sp, low_row[:, :], dr["low_row"], in_g)
            dma_in(sp, X[:, :, :], dr["x"], in_res)
            stack(1, 1, 1)
            mem["load_later"](sp)
            for b in range(2, NB):
                stack(b, b, b % 2)
            mem["wait_later"](sp)

        @block.gpsimd
        def _(pool):
            pool.memset(neg_half[:, :], -0.5).then_inc(consts, 1)
            pool.memset(one_col[:, :], 1.0).then_inc(consts, 1)
            pool.sem_inc(sq_done, 2)
            pool.sem_inc(y_ready, 4)
            pool.sem_inc(y_copied, 2)

            def split_x(b, v, par):
                pool.wait_ge((in_x0, in_x1)[v] if v < 2 else in_x, 16)
                if v >= 2:
                    pool.wait_ge(pj_ready, (b - 1) * 8)
                src = xT[:, bass.ds(b * L, L)] if not isinstance(b, int) else xT[:, b * L:(b + 1) * L]
                pool.tensor_scalar(xs_h[:, par, :], src, 1.0, 0.0, ALU.mult, ALU.add).then_inc(xs_hi, 1)
                pool.wait_ge(xs_hi, b + 1)
                pool.tensor_tensor(xs_l[:, par, :], src, xs_h[:, par, :].bitcast(F32), ALU.subtract).then_inc(xs_ready, 1)

            split_x(0, 0, 0)
            split_x(1, 1, 1)

            def square(b, v, j):
                n = b * NPAIR + j
                pool.wait_ge(y_copied, n + 1 + 2)
                if v >= 2 and j == 0:
                    pool.wait_ge(mi_ready, MI_OF(b) - 4 if v > 2 else 1)
                pool.tensor_tensor(Y2[:, v % 2, j, :], Y[:, v % 2, j, :], Y[:, v % 2, j, :], ALU.mult).then_inc(y2_ready, 1)

            def step(b, v):
                for j in range(NPAIR):
                    if lagged(b, v, j):
                        square(*lagged(b, v, j))
                    if j == 2 and 2 <= v:
                        pool.wait_ge(ve_ready, b - 1)
                        pool.tensor_tensor(rs[:, :], ve[:, :], neg_half[:, 0:2], ALU.pow).then_inc(rs_ready, 1)
                    if j == 6 and v + 2 < NB:
                        split_x(b + 2, v + 2, v % 2)

            for b in range(NB + 2):
                step(b, b)
                if b == 0:
                    pool.wait_ge(in_o, 16)
                    pool.wait_ge(in_g, 32)
                    pool.tensor_scalar(w_og[:, :, :], w_o[:, :, :], g_col[:, 0:1], 1.0, ALU.mult, ALU.mult).then_inc(consts, 1)
                if b in (3, 4, 5):
                    if b == 3:
                        pool.wait_ge(mem["in_w1"], 16)
                    e = b - 3
                    split_on_pool(pool, mem["w1"][:, e, :], mem["w1_h"][:, e, :], mem["w1_l"][:, e, :], w_step, e, mem["w_split"])

        @block.scalar
        def _(act):
            def evacuate(b, v, u):
                act.wait_ge(pj_ready, b * 8 + u + 1)
                if u < 4:
                    if u == 0 and v >= 1:
                        act.wait_ge(stacked, 128 * b)
                    act.activation(c_h[:, u // 2, (u % 2) * L:(u % 2 + 1) * L], proj_bank(v, u)[:, 0:L], ACT.Copy).then_inc(hi_ready, 1)
                else:
                    t, half = divmod(u - 4, 2)
                    act.activation(V[:, v % 2, t, half * 512:(half + 1) * 512], proj_bank(v, u)[:, :], ACT.Copy).then_inc(pj_read, 1)

            def copy_y(b, v, j):
                act.wait_ge(y_ready, b * NPAIR + j + 1 + 4)
                act.activation(Y[:, v % 2, j, :], YP[j % 2][:, 0:L], ACT.Copy).then_inc(y_copied, 1)

            def step(b, v):
                for j in range(NPAIR):
                    if v < NB:
                        n = b * NPAIR + j
                        act.wait_ge(s_ready, n + 1)
                        act.wait_ge(y_ready, n + 1)
                        act.activation(UA[:, j % 4, :, :], S[j % 2][:, :, 0:SW], ACT.Square,
                                       bias=one_col[:, 0:1], scale=0.25).then_inc(sq_done, 1)
                    if j == 3 and 1 <= v <= NB:
                        act.wait_ge(mi_read, MI_OF(b) + 2 if v > 1 else 1)
                        act.activation(rms[:, :], ms[:, :], ACT.Sqrt).then_inc(rms_ready, 1)
                    if lagged(b, v, j):
                        copy_y(*lagged(b, v, j))
                    if v + 1 < NB:
                        evacuate(b + 1, v + 1, j)
                    if v == NB - 1 and j == 1:
                        gate_high(act, mem, 0, 1, PJ)
                    if v == NB - 1 and j == 2:
                        gate_full(act, mem, 0, PJ, w_v[:, 0:BT])
                    if v == NB - 1 and j == 7:
                        gate_high(act, mem, 0, 0, PJ)

            act.wait_ge(consts, 2)
            act.activation(warm[:, :], one_col[:, :], ACT.Square).then_inc(warm_done, 1)
            for u in range(8):
                evacuate(0, 0, u)
            for b in range(NB + 1):
                step(b, b)

        @block.vector
        def _(dve):
            for n, (w, h, l, loaded) in enumerate(((w_qk, qk_h, qk_l, in_wqk), (w_v, v_h, v_l, in_wv))):
                dve.wait_ge(loaded, 16)
                full = (slice(None),) * len(w.shape)
                dve.tensor_copy(h[full], w[full]).then_inc(w_split, 1)
                dve.wait_ge(w_split, 2 * n + 1)
                dve.tensor_tensor(l[full], w[full], h[full].bitcast(F32), ALU.subtract).then_inc(w_split, 1)

            def low(b, v, u):
                dve.wait_ge(hi_ready, b * 4 + u + 1)
                out = slice((u % 2) * L, (u % 2 + 1) * L)
                dve.tensor_tensor(c_l[:, u // 2, out], proj_bank(v, u)[:, 0:L], c_h[:, u // 2, out].bitcast(F32),
                                  ALU.subtract).then_inc(lo_ready, 1)

            def norm(b, v):
                e = MI_OF(b + 2)
                dve.wait_ge(mi_ready, e + 1)
                if v == 0:
                    dve.wait_ge(in_res, 16)
                x = X[:, 2 * b:2 * b + 2, :] if isinstance(b, int) else X[:, bass.ds(2 * b, 2), :]
                dve.tensor_tensor(RES[:, v % 2, :, :], MI[:, 0:2 * D].rearrange("p (t d) -> p t d", t=2), x, ALU.add).then_inc(mi_read, 1)
                dve.wait_ge(mi_read, e + 1)
                for t in range(2):
                    i = dve.bn_stats(st[:, t, :], RES[:, v % 2, t, :])
                i.then_inc(ln_step, 1)
                dve.wait_ge(ln_step, 2 * b + 1)
                for t in range(2):
                    i = dve.bn_aggr(mv[:, t, :], st[:, t, :])
                i.then_inc(ln_step, 1)
                dve.wait_ge(ln_step, 2 * b + 2)
                dve.tensor_scalar(ve[:, :], mv[:, :, 1], LN_EPS, None, ALU.add).then_inc(ve_ready, 1)

            def norm_end(b, v):
                dve.wait_ge(rs_ready, b + 1)
                for t in range(2):
                    out = X[:, 2 * b + t, :]
                    i = dve.tensor_scalar(out, RES[:, v % 2, t, :], mv[:, t, 0:1], rs[:, t:t + 1], ALU.subtract, ALU.mult)
                i.then_inc(x_done, 1)

            def scale(b, v, g):
                e = MI_OF(b) + 2 + g if v > 1 else 1 + g
                dve.wait_ge(mi_ready, e + 1)
                dve.tensor_tensor(YN[:, 2 * g:2 * g + 2, :], spread_bank(v, g).rearrange("p (j n) -> p j n", j=2),
                                  Y[:, (v - 1) % 2, 2 * g:2 * g + 2, :], ALU.mult).then_inc(mi_read, 1)

            def step(b, v):
                for j in range(NPAIR):
                    if j == 3 and 1 <= v <= NB:
                        e = MI_OF(b) + 1 if v > 1 else 0
                        dve.wait_ge(mi_ready, e + 1)
                        dve.tensor_scalar(ms[:, :], MI[:, 0:L], 1.0 / E0, 4 * RMS_EPS, ALU.mult, ALU.add).then_inc(mi_read, 1)
                    if j == 4 and 1 <= v <= NB:
                        if v == 1:
                            dve.wait_ge(in_g, 32)
                        dve.wait_ge(rms_ready, b)
                        dve.reciprocal(rr[:, :], rms[:, :]).then_inc(rr_ready, 1)
                        dve.wait_ge(rr_ready, b)
                        dve.tensor_copy(rr_h[:, :], rr[:, :]).then_inc(rr_hi, 1)
                        dve.wait_ge(rr_hi, b)
                        dve.scalar_tensor_tensor(rr_parts[:, :], rr_h[:, :].bitcast(F32), low_row[:, 0:1], rr[:, :], ALU.mult, ALU.add).then_inc(rr_split, 1)
                    if v < NB:
                        n = b * NPAIR + j
                        dve.wait_ge(sq_done, n + 1 + 2)
                        dve.scalar_tensor_tensor(UA[:, j % 4, :, :], UA[:, j % 4, :, :], 1.0,
                                                 mask[:, None, :].to_broadcast([P, 2, SW]), ALU.add, ALU.mult).then_inc(a_ready, 1)
                    if v + 1 < NB and j < 4:
                        low(b + 1, v + 1, j)
                    if j == 1 and v >= 2:
                        norm(b - 2, v - 2)
                    if j == 3 and v >= 2:
                        norm_end(b - 2, v - 2)
                    if spread_at(b, v, j):
                        scale(*spread_at(b, v, j))
                    if v == NB - 1 and j == 1:
                        gate_low(dve, mem, 0, 1, PJ)
                    if v == NB - 1 and j == 4:
                        gate_choose(dve, mem, 0, PJ)
                    if v == NB and j == 1:
                        gate_low(dve, mem, 0, 0, PJ)

            for u in range(4):
                low(0, 0, u)
            dve.wait_ge(in_mask, 16)
            for b in range(NB + 2):
                step(b, b)
                if b == 0:
                    dve.wait_ge(in_c, 32)
                    dve.tensor_copy(exp_sel[:, :, :], exp_selw[:, :, :]).then_inc(w_split, 1)

        @block.tensor
        def _(pe):
            def project(b, v, u):
                if u == 0:
                    pe.wait_ge(xs_ready, b + 1)
                if v == 0:
                    pe.wait_ge(w_split, 2 if u < 4 else 4)
                elif u == 0:
                    pe.wait_ge(pj_read, 4 * b)
                elif u <= 4:
                    pe.wait_ge(lo_ready, 4 * b + u)
                else:
                    pe.wait_ge(pj_read, 4 * b + u - 4)
                xh, xl = xs_h[:, v % 2, :], xs_l[:, v % 2, :]
                if u < 4:
                    i = three_pass(pe, proj_bank(v, u)[:, 0:L], qk_h[:, u, :], qk_l[:, u, :], xh, xl)
                else:
                    t, half = divmod(u - 4, 2)
                    tt, hh = slice(t * P, (t + 1) * P), slice(half * 512, (half + 1) * 512)
                    i = three_pass(pe, proj_bank(v, u)[:, :], xs_h[:, v % 2, tt], xs_l[:, v % 2, tt], v_h[:, hh], v_l[:, hh])
                i.then_inc(pj_ready, 1)

            def scores(b, v, j):
                n = b * NPAIR + j
                if j == 0:
                    pe.wait_ge(stacked, 128 * (b + 1))
                pe.wait_ge(sq_done, n + 1)
                for par in range(2):
                    rows = slice(64 * par, 64 * par + 64)
                    kk, qq = k4[rows, v % 2, j * L:(j + 1) * L], q4[rows, v % 2, j * L:(j + 1) * L]
                    pe.matmul(S[j % 2][:, par, 0:L], kk[:, 0:P], qq[:, 0:L], start=True, stop=True)
                    i = pe.matmul(S[j % 2][:, par, L:SW], kk[:, P:L], qq[:, P:L], start=True, stop=True)
                i.then_inc(s_ready, 1)

            def attend(b, v, j):
                n = b * NPAIR + j
                pe.wait_ge(a_ready, n + 1)
                pe.wait_ge(y_copied, n + 1)
                if n == 0:
                    pe.wait_ge(pj_read, 4)
                for t in range(2):
                    for par in range(2):
                        h = 2 * j + par
                        cols = slice(0, L) if t == 0 else slice(L, SW)
                        i = pe.matmul(YP[j % 2][64 * par:64 * par + 64, t * P:L], V[:, v % 2, t, h * E0:(h + 1) * E0],
                                      UA[:, j % 4, par, cols], start=(t == 0), stop=(t == 1), skip_group_check=True)
                i.then_inc(y_ready, 1)

            def spread(b, v, g):
                if v < NB:
                    pe.wait_ge(mi_read, MI_OF(b) + 2 + g if v > 1 else 1 + g)
                else:
                    pe.wait_ge(sq_done, NB * NPAIR + 2)
                if v == NB and g == 0:
                    pe.wait_ge(mem["f0_xl_ready"], 2)
                    for _ in range(16):
                        pe.matmul(PJ[:, 0:L], qk_h[:, 0, :], xs_h[:, 0, :], start=True, stop=True)
                if g == 0:
                    pe.wait_ge(rr_split, b)
                if v == 1 and g == 0:
                    pe.wait_ge(w_split, 5)
                for k in range(2):
                    out = spread_bank(v, g)[:, k * L:(k + 1) * L]
                    i = pe.matmul(out, exp_sel[:, 2 * g + k, :], rr_parts[:, :], start=(k == 0), stop=True, skip_group_check=True)
                i.then_inc(mi_ready, 1)

            def step(b, v):
                for j in range(NPAIR):
                    if v < NB:
                        scores(b, v, j)
                    if lagged(b, v, j):
                        attend(*lagged(b, v, j))
                    if v + 1 < NB:
                        project(b + 1, v + 1, j)
                    if v == NB - 1 and j == 0:
                        pe.wait_ge(in_f0, 80)
                        pe.wait_ge(x_done, TB // 2)
                        pe.wait_ge(pj_read, 4 * NB)
                        gate_transpose(pe, mem, 0, PJ)
                    if v == NB - 1 and j == 3:
                        gate_scores(pe, mem, 0, w_v[:, 0:BT], PJ)
                    if v == NB - 1 and j == 6:
                        gate_transpose_x0(pe, mem, 0, PJ)
                    if spread_at(b, v, j):
                        spread(*spread_at(b, v, j))
                    if j == 1 and v >= 2:
                        if v == 2:
                            pe.wait_ge(consts, 3)
                        pe.wait_ge(mi_read, MI_OF(b))
                        for t in range(2):
                            for k in range(NPAIR):
                                i = pe.matmul(MI[:, t * D:(t + 1) * D], YN[:, k, t * P:(t + 1) * P], w_og[:, k, :],
                                              start=(k == 0), stop=(k == NPAIR - 1))
                        i.then_inc(mi_ready, 1)
                    if j == 2 and 1 <= v <= NB:
                        e = MI_OF(b) + 1 if v > 1 else 0
                        pe.wait_ge(mi_read, e)
                        pe.wait_ge(y2_ready, b * NPAIR)
                        for k in range(NPAIR):
                            q = 32 * (k % 4)
                            i = pe.matmul(MI[q:q + 32, 0:L], sum_sel[:, k, :], Y2[:, (v - 1) % 2, k, :],
                                          start=(k < 4), stop=(k >= 4), skip_group_check=True)
                        i.then_inc(mi_ready, 1)
            for u in range(8):
                project(0, 0, u)
            for b in range(NB + 2):
                step(b, b)
        mem["x_done"], mem["before"] = (x_done, NB), (mi_ready, MI_OF(NB + 1) + 1)


def norm_stats(dve, res, stats, mv, var, tiles, step, done, ready):
    for t in range(tiles):
        i = dve.bn_stats(stats[:, t, :], res[:, t, :])
    i.then_inc(step, 1)
    dve.wait_ge(step, done + 1)
    for t in range(tiles):
        i = dve.bn_aggr(mv[:, t, :], stats[:, t, :])
    i.then_inc(step, 1)
    dve.wait_ge(step, done + 2)
    dve.tensor_scalar(var[:, 0:tiles], mv[:, 0:tiles, 1], LN_EPS, None, ALU.add).then_inc(ready, 1)


def norm_apply(dve, out, res, mv, rstd, tiles):
    for t in range(tiles):
        i = dve.tensor_scalar(out[:, t, :], res[:, t, :], mv[:, t, 0:1], rstd[:, t:t + 1], ALU.subtract, ALU.mult)
    return i


def split_on_pool(pool, src, hi, lo, step, done, ready):
    pool.tensor_scalar(hi, src, 1.0, 0.0, ALU.mult, ALU.add).then_inc(step, 1)
    pool.wait_ge(step, done + 1)
    pool.tensor_tensor(lo, src, hi.bitcast(F32), ALU.subtract).then_inc(ready, 1)



def gate_transpose(pe, mem, i, bank):
    for t in range(TB):
        k = pe.transpose(bank[:, t * P:(t + 1) * P], mem["X"][:, TB * i + t, :], mem["ident"][:, :])
    k.then_inc(mem["f0_t_ready"], 1)


def gate_high(act, mem, i, part, bank):
    act.wait_ge(mem["f0_t_ready"], 2 * i + (1 if part == 1 else 2))
    act.activation(mem["f0_xh"][i % 2][part], bank[:, :], ACT.Copy).then_inc(mem["f0_xh_ready"], 1)


def gate_low(dve, mem, i, part, bank):
    dve.wait_ge(mem["f0_xh_ready"], 2 * i + (1 if part == 1 else 2))
    dve.tensor_tensor(mem["f0_xl"][i % 2][part], bank[:, :], mem["f0_xh"][i % 2][part].bitcast(F32), ALU.subtract).then_inc(mem["f0_xl_ready"], 1)


def gate_full(act, mem, i, bank, xT):
    act.wait_ge(mem["f0_xl_ready"], 2 * i + 1)
    if i >= 1:
        act.wait_ge(mem["f0_gate_ready"], i)
    act.activation(xT, bank[:, :], ACT.Copy).then_inc(mem["f0_xT_ready"], 1)


def gate_scores(pe, mem, i, xT, bank):
    pe.wait_ge(mem["f0_xT_ready"], i + 1)
    if i >= 1:
        pe.wait_ge(mem["f0_sc_ready"], i)
    for t in range(TB):
        k = pe.matmul(bank[:, 2 * t:2 * t + 2], xT[:, t * P:(t + 1) * P], mem["gate_w"][:, :], start=True, stop=True)
    k.then_inc(mem["f0_gate_ready"], 1)


def gate_choose(dve, mem, i, bank):
    dve.wait_ge(mem["f0_gate_ready"], i + 1)
    dve.tensor_copy(mem["f0_sc"][:, :, :], bank[:, 0:2 * TB].rearrange("p (t e) -> p t e", e=2)).then_inc(mem["f0_sc_ready"], 1)
    dve.wait_ge(mem["f0_sc_ready"], i + 1)
    dve.tensor_tensor(mem["f0_pick0"][:, :], mem["f0_sc"][:, :, 0], mem["f0_sc"][:, :, 1], ALU.is_ge).then_inc(mem["f0_pick_ready"], 1)
    dve.wait_ge(mem["f0_pick_ready"], i + 1)
    if i >= 1:
        dve.wait_ge(mem["f0_xh_ready"], 2 * i)
    for t in range(TB):
        k = dve.tensor_scalar(mem["f0_x0"][:, t * D:(t + 1) * D], mem["X"][:, TB * i + t, :], mem["f0_pick0"][:, t:t + 1], None, ALU.mult)
    k.then_inc(mem["f0_x0_ready"], 1)


def gate_transpose_x0(pe, mem, i, bank):
    pe.wait_ge(mem["f0_x0_ready"], i + 1)
    for t in range(TB):
        k = pe.transpose(bank[:, t * P:(t + 1) * P], mem["f0_x0"][:, t * D:(t + 1) * D], mem["ident"][:, :])
    k.then_inc(mem["f0_t_ready"], 1)


def feed_forward0(nc, mem, dr):
    X = mem["X"]
    NC = NE0 * HC
    ctx = ExitStack()
    with ctx:
        sb = lambda n, s, d=F32: ctx.enter_context(nc.sbuf_tensor(n, s, d))
        sem = lambda n: mem["scope"].enter_context(nc.semaphore("f0_" + n))
        w1_h, w1_l, w2 = mem["w1_h"], mem["w1_l"], mem["w2"]
        b1, b2 = mem["b1"], mem["b2"]
        b_sum = sb("f0_bsum", [P, 2, D])
        xb = sb("f0_xb", [P, 2, TB, D])
        xT = mem["xT"][:, :, :].rearrange("p a n -> p (a n)")
        xh, xl = mem["f0_xh"], mem["f0_xl"]
        for parts, name in ((xh, "h"), (xl, "l")):
            parts[0][2] = sb(f"f0_x{name}02", [P, BT], F32R)[:, :]
            for e in range(NE0):
                parts[1][e] = sb(f"f0_x{name}1{e}", [P, BT], F32R)[:, :]
        hid = sb("f0_hid", [P, 2, NC, BT])
        res = [mem["RES"][:, :, :, :].rearrange("p a b d -> p (a b) d"), mem["a1_wqk"][:, :].rearrange("p (t d) -> p t d", d=D)]
        stats = sb("f0_stats", [P, TB, 6])
        mv = sb("f0_mv", [P, 2, TB, 2])
        var = sb("f0_var", [P, TB])
        rstd = sb("f0_rstd", [P, TB])
        neg_half = sb("f0_neghalf", [P, TB])
        T = [ctx.enter_context(nc.psum_tensor(f"f0_T{i}", [P, 512], F32)) for i in range(2)]
        G = ctx.enter_context(nc.psum_tensor("f0_G", [P, 512], F32))
        HP = [ctx.enter_context(nc.psum_tensor(f"f0_H{i}", [P, 512], F32)) for i in range(3)]
        O = [ctx.enter_context(nc.psum_tensor(f"f0_O{i}", [P, 512], F32)) for i in range(2)]
        bias_step, bias_ready, xb_ready = sem("bias_step"), sem("bias_ready"), sem("xb_ready")
        xl_ready, sc_ready, x_done = mem["f0_xl_ready"], mem["f0_sc_ready"], sem("x_done")
        x1h_ready, x1l_ready = sem("x1h_ready"), sem("x1l_ready")
        h_ready = sem("h_ready")
        h_act, h_dve = sem("h_act"), sem("h_dve")
        o_ready = sem("o_ready")
        res_ready, ln_step, var_ready, rstd_ready = (sem(n) for n in "res_ready ln_step var_ready rstd_ready".split())
        consts, split_step = sem("consts"), sem("split_step")
        block, before, x_final = mem["block"], mem["before"], mem["x_done"]

        @block.sync
        def _(sp):
            sp.wait_ge(*before)
            mem["load_layer1"](sp)
            prep_stack(sp, mem, 0, 0)
            prep_stack(sp, mem, 0, 1)

        @block.gpsimd
        def _(pool):
            pool.wait_ge(*before)
            pool.memset(neg_half[:, :], -0.5).then_inc(consts, 1)
            pool.memset(mem["zero_rows"][:, :], 0.0)
            pool.memset(mem["neg_rows"][:, :], -1.0)
            splits = 0
            for i in range(NBLK):
                p = i % 2
                pool.wait_ge(xl_ready, 2 * i + 2)
                pool.tensor_tensor(xh[p][2], xh[p][1].bitcast(F32), xh[p][0].bitcast(F32), ALU.subtract).then_inc(x1h_ready, 1)
                pool.tensor_tensor(xl[p][2], xl[p][1].bitcast(F32), xl[p][0].bitcast(F32), ALU.subtract).then_inc(x1l_ready, 1)
                if i == 0:
                    pool.tensor_tensor(b_sum[:, 0, :], b2[:, 0, :], b2[:, 1, :], ALU.add).then_inc(bias_step, 1)
                    pool.wait_ge(bias_step, 1)
                    pool.tensor_tensor(b_sum[:, 1, :], b_sum[:, 0, :], b2[:, 2, :], ALU.add).then_inc(bias_ready, 1)
                    pool.wait_ge(bias_ready, 1)
                if i >= 2:
                    pool.wait_ge(res_ready, i - 1)
                if i == NBLK - 1:
                    pool.wait_ge(*x_final)
                pool.tensor_tensor(xb[:, p, :, :], X[:, TB * i:TB * i + TB, :],
                                   b_sum[:, 1:2, :].to_broadcast([P, TB, D]), ALU.add).then_inc(xb_ready, 1)
                if i >= 2:
                    pool.wait_ge(var_ready, i - 1)
                    pool.tensor_tensor(rstd[:, :], var[:, :], neg_half[:, :], ALU.pow).then_inc(rstd_ready, 1)
                if i == 0:
                    pool.memset(mem["q4"][0][:, :].bitcast(F32), 0.0).then_inc(mem["zeroed"], 1)
                    pool.memset(mem["k4"][0][:, :].bitcast(F32), 0.0).then_inc(mem["zeroed"], 1)
                if i == NBLK - 1:
                    prep_sum(pool, mem, 0, 0)
                    prep_sum(pool, mem, 0, 1)
                for src, hi, lo, loaded, cols in mem["splits"][i]:
                    pool.wait_ge(loaded, 16)
                    for c in range(0, cols, 512):
                        split_on_pool(pool, src[:, c:c + 512], hi[:, c:c + 512], lo[:, c:c + 512], split_step, splits, mem["w_split"])
                        splits += 1
            prep_low(pool, mem, 0, 0)
            prep_low(pool, mem, 0, 1)
            for i in range(NBLK - 2, NBLK):
                if i == NBLK - 1:
                    for t in range(2):
                        prep_sum(pool, mem, 1, t)
                        prep_low(pool, mem, 1, t)
                pool.wait_ge(var_ready, i + 1)
                pool.tensor_tensor(rstd[:, :], var[:, :], neg_half[:, :], ALU.pow).then_inc(rstd_ready, 1)

        @block.scalar
        def _(act):
            act.wait_ge(*before)

            def prepare(i, part):
                if i >= 2 and part == 0:
                    act.wait_ge(h_ready, (i - 1) * NC)
                if part == 0:
                    gate_high(act, mem, i, 1, T[0])
                    gate_full(act, mem, i, T[0], xT)
                else:
                    gate_high(act, mem, i, 0, T[1])

            for i in range(NBLK):
                for c in range(0, NC, 2):
                    act.wait_ge(h_ready, i * NC + c + 1)
                    if i >= 2 and c == 0:
                        act.wait_ge(o_ready, i - 1)
                    act.activation(hid[:, i % 2, c, :], HP[(i * NC + c) % 3][:, :], ACT.Relu, bias=b1[:, c:c + 1]).then_inc(h_act, 1)
                    if i + 1 < NBLK and c in (2, 8):
                        prepare(i + 1, (c - 2) // 6)
                    if i == NBLK - 1:
                        if c in (0, 6):
                            prep_x_high(act, mem, c // 6, T[0])
                        if c in (2, 8):
                            prep_x_full(act, mem, c // 6, T[0])
                        if c in (8, 10):
                            prep_high(act, mem, 0, (c - 8) // 2)
            for t in range(2):
                prep_high(act, mem, 1, t)

        @block.vector
        def _(dve):
            dve.wait_ge(*before)
            def prepare(i, part):
                if part == 0:
                    gate_low(dve, mem, i, 1, T[0])
                    gate_choose(dve, mem, i, G)
                else:
                    gate_low(dve, mem, i, 0, T[1])

            def residual(i):
                dve.wait_ge(o_ready, i + 1)
                dve.wait_ge(xb_ready, i + 1)
                if i == 1:
                    dve.wait_ge(mem["w_split"], NE0 + 1)
                dve.tensor_tensor(res[i % 2], O[i % 2][:, :].rearrange("p (t d) -> p t d", t=TB), xb[:, i % 2, :, :], ALU.add).then_inc(res_ready, 1)
                dve.wait_ge(res_ready, i + 1)
                norm_stats(dve, res[i % 2], stats, mv[:, i % 2], var, TB, ln_step, 2 * i, var_ready)

            def finish(i):
                dve.wait_ge(rstd_ready, i + 1)
                norm_apply(dve, X[:, TB * i:TB * i + TB, :], res[i % 2], mv[:, i % 2], rstd, TB).then_inc(x_done, 1)

            for i in range(NBLK + 1):
                for c in range(1, NC, 2):
                    if i < NBLK:
                        dve.wait_ge(h_ready, i * NC + c + 1)
                        dve.tensor_scalar(hid[:, i % 2, c, :], HP[(i * NC + c) % 3][:, :], b1[:, c:c + 1], 0.0, ALU.add, ALU.max).then_inc(h_dve, 1)
                    if i + 1 < NBLK and c in (3, 9):
                        prepare(i + 1, (c - 3) // 6)
                    if i == NBLK - 1:
                        b, k = divmod(c // 2, 3)
                        if k == 0:
                            prep_x_low(dve, mem, b, T[0])
                        else:
                            if b == 0 and k == 1:
                                dve.wait_ge(*mem["rope_loaded"])
                            prep_rotate(dve, mem, b, k - 1, (T[1], G)[k - 1])
                    if c == 1 and i >= 2:
                        residual(i - 2)
                    if c == 7 and i >= 2:
                        finish(i - 2)
            residual(NBLK - 1)
            finish(NBLK - 1)

        @block.tensor
        def _(pe):
            pe.wait_ge(*before)
            def prepare(i, part):
                if part == 0:
                    if i == NBLK - 1:
                        pe.wait_ge(*x_final)
                    pe.wait_ge(mem["f0_xT_ready"], i)
                    gate_transpose(pe, mem, i, T[0])
                elif part == 1:
                    gate_scores(pe, mem, i, xT, G)
                else:
                    pe.wait_ge(xl_ready, 2 * i)
                    gate_transpose_x0(pe, mem, i, T[1])

            def up(i, c):
                n, e, p = i * NC + c, c // HC, i % 2
                if n >= 3:
                    pe.wait_ge(h_act if (n - 3) % 2 == 0 else h_dve, (n - 3) // 2 + 1)
                if c == 0:
                    pe.wait_ge(xl_ready, 2 * i + 2)
                if e == 2 and c % HC == 0:
                    pe.wait_ge(x1l_ready, i + 1)
                    pe.wait_ge(x1h_ready, i + 1)
                cols = slice((c % HC) * P, (c % HC + 1) * P)
                three_pass(pe, HP[n % 3][:, :], w1_h[:, e, cols], w1_l[:, e, cols], xh[p][e], xl[p][e]).then_inc(h_ready, 1)

            def down(i, s):
                t, third = divmod(s, 3)
                if s == 0 and i >= 2:
                    pe.wait_ge(res_ready, i - 1)
                if s < 3:
                    pe.wait_ge(h_act, i * NC // 2 + 2 * (third + 1))
                    pe.wait_ge(h_dve, i * NC // 2 + 2 * (third + 1))
                for c in range(4 * third, 4 * third + 4):
                    k = pe.matmul(O[i % 2][:, t * D:(t + 1) * D], hid[:, i % 2, c, t * P:(t + 1) * P], w2[:, c, :],
                                  start=(c == 0), stop=(c == NC - 1))
                if s == NC - 1:
                    k.then_inc(o_ready, 1)

            for i in range(NBLK + 1):
                for c in range(NC):
                    if i < NBLK:
                        up(i, c)
                    if i >= 1:
                        down(i - 1, c)
                    if i + 1 < NBLK and c in (2, 5, 8):
                        prepare(i + 1, (c - 2) // 3)
                    if i == NBLK - 1 and c % 2 == 0:
                        b, k = divmod(c // 2, 3)
                        if k == 0:
                            pe.wait_ge(x_done, 1)
                            if b == 0:
                                pe.wait_ge(mem["f0_xT_ready"], NBLK)
                            else:
                                pe.wait_ge(mem["xT_ready"], b)
                            prep_transpose(pe, mem, b, T[0])
                        else:
                            if b == 0 and k == 1:
                                pe.wait_ge(mem["w_split"], NE0 + 1)
                                pe.wait_ge(xl_ready, 2 * NBLK)
                            elif b == 0:
                                pe.wait_ge(sc_ready, NBLK)
                            else:
                                pe.wait_ge(mem["rb_ready"], 2 * (b - 1) + k)
                            prep_project(pe, mem, b, k - 1, (T[1], G)[k - 1])
        mem["x_done"], mem["before"] = (x_done, NBLK), (res_ready, NBLK)


BUFS = 4


def prep_transpose(pe, mem, b, bank):
    for t in range(2):
        i = pe.transpose(bank[:, t * P:(t + 1) * P], mem["X"][:, 2 * b + t, :], mem["ident"][:, :])
    i.then_inc(mem["xt_ready"], 1)


def prep_x_high(act, mem, b, bank):
    act.wait_ge(mem["xt_ready"], b + 1)
    if b >= 2:
        act.wait_ge(mem["v_ready"], b - 1)
    act.activation(mem["xh"][:, b % 2, :], bank[:, 0:L], ACT.Copy).then_inc(mem["xh_ready"], 1)


def prep_x_low(dve, mem, b, bank):
    dve.wait_ge(mem["xh_ready"], b + 1)
    dve.tensor_tensor(mem["xl"][:, b % 2, :], bank[:, 0:L], mem["xh"][:, b % 2, :].bitcast(F32), ALU.subtract).then_inc(mem["xl_ready"], 1)


def prep_x_full(act, mem, b, bank):
    act.wait_ge(mem["xl_ready"], b + 1)
    act.activation(mem["xT"][:, b % 2, :], bank[:, 0:L], ACT.Copy).then_inc(mem["xT_ready"], 1)


def prep_project(pe, mem, b, t, bank):
    pe.wait_ge(mem["xl_ready"], b + 1)
    for s in range(2):
        cols = slice((2 * t + s) * P, (2 * t + s + 1) * P)
        i = three_pass(pe, bank[:, s * L:(s + 1) * L], mem["a1_wqk_h"][:, cols], mem["a1_wqk_l"][:, cols],
                       mem["xh"][:, b % 2, :], mem["xl"][:, b % 2, :])
    i.then_inc(mem["qk_ready"], 1)


def prep_rotate(dve, mem, b, t, bank):
    dve.wait_ge(mem["qk_ready"], 2 * b + t + 1)
    if b >= 1:
        dve.wait_ge(mem["rq_ready"], 2 * (b - 1) + t + 1)
    dve.tensor_tensor(mem["ra"][:, t, :], bank[:, 0:L], mem["rope"][:, 0, :], ALU.mult).then_inc(mem["ra_ready"], 1)
    dve.tensor_tensor(mem["rb"][:, t, :], bank[:, L:2 * L], mem["rope"][:, 1, :], ALU.mult).then_inc(mem["rb_ready"], 1)


def prep_sum(pool, mem, b, t):
    pool.wait_ge(mem["ra_ready"], 2 * b + t + 1)
    pool.wait_ge(mem["rb_ready"], 2 * b + t + 1)
    if b >= 1:
        pool.wait_ge(mem["cl_ready"], 2 * b)
    pool.tensor_tensor(mem["rq"][:, t, :], mem["ra"][:, t, :], mem["rb"][:, t, :], ALU.add).then_inc(mem["rq_ready"], 1)


def prep_high(act, mem, b, t):
    act.wait_ge(mem["rq_ready"], 2 * b + t + 1)
    if b >= 1:
        act.wait_ge(mem["stacked"], stacked_by(b - 1))
    act.activation(mem["c_h"][:, t, :], mem["rq"][:, t, :], ACT.Copy).then_inc(mem["ch_ready"], 1)


def prep_low(pool, mem, b, t):
    pool.wait_ge(mem["ch_ready"], 2 * b + t + 1)
    pool.tensor_tensor(mem["c_l"][:, t, :], mem["rq"][:, t, :], mem["c_h"][:, t, :].bitcast(F32), ALU.subtract).then_inc(mem["cl_ready"], 1)


def prep_fixed(sp, mem, n):
    sp.wait_ge(mem["zeroed"], 2 * (n + 1) if n < 2 else 2 * BUFS)
    sp.dma_start(mem["k4"][n][4:P:32, :].bitcast(F32), mem["neg_rows"][:, :]).then_inc(mem["fixed"][n], 16)
    sp.dma_start(mem["q4"][n][4:P:32, :].bitcast(F32), mem["zero_rows"][:, :]).then_inc(mem["fixed"][n], 16)


def prep_stack(sp, mem, b, t):
    n, c_h, c_l = b % BUFS, mem["c_h"], mem["c_l"]
    dst, parts = ((mem["q4"][n], (c_h, c_h, c_l, c_l)), (mem["k4"][n], (c_h, c_l, c_h, c_l)))[t]
    if b >= BUFS and t == 0:
        sp.dma_start(dst[4:P:32, :].bitcast(F32), mem["zero_rows"][:, :]).then_inc(mem["stacked"], 16)
    sp.wait_ge(mem["cl_ready"], 2 * b + t + 1)
    for c in range(4):
        sp.dma_start(dst[c:P:8, :].bitcast(F32), parts[c][:, t, :].bitcast(F32)).then_inc(mem["stacked"], 16)


def stacked_by(b):
    return 16 * (8 * (b + 1) + max(0, b + 1 - BUFS))


def block_transpose(pe, mem, i, bank):
    for t in range(TB):
        k = pe.transpose(bank[:, t * P:(t + 1) * P], mem["X"][:, TB * i + t, :], mem["ident"][:, :])
    k.then_inc(mem["bt_ready"], 1)


def block_high(act, mem, i, bank):
    act.wait_ge(mem["bt_ready"], i + 1)
    act.activation(mem["bxh"][i % 2], bank[:, :], ACT.Copy).then_inc(mem["bxh_ready"], 1)


def block_low(dve, mem, i, bank):
    dve.wait_ge(mem["bxh_ready"], i + 1)
    dve.tensor_tensor(mem["bxl"][i % 2], bank[:, :], mem["bxh"][i % 2].bitcast(F32), ALU.subtract).then_inc(mem["bxl_ready"], 1)


def block_full(act, mem, i, bank):
    act.wait_ge(mem["bxl_ready"], i + 1)
    act.activation(mem["bxT"], bank[:, :], ACT.Copy).then_inc(mem["bxT_ready"], 1)


def attention1(nc, mem, dr):
    X = mem["X"]
    NH = NB * H1
    AHEAD = 24
    ctx = ExitStack()
    with ctx:
        sb = lambda n, s, d=F32: ctx.enter_context(nc.sbuf_tensor("a1_" + n, s, d))
        sem = lambda n: mem["scope"].enter_context(nc.semaphore("a1_" + n))
        ident = mem["ident"]
        xT, q4, k4 = mem["xT"], mem["q4"], mem["k4"]
        for n in range(1, BUFS):
            q4.append(sb(f"q4_{n}", [P, NPAIR * L], F32R))
            k4.append(sb(f"k4_{n}", [P, NPAIR * L], F32R))
        V1 = sb("V1", [P, 4, 2, H1, 32])
        m3 = sb("m3", [P, 2, H1, 3])
        mm = sb("mm", [P, 2, H1])
        mx = sb("mx", [P, 2, 2, 2, NPAIR], F32R)
        mT = sb("mT", [32, L], F32R)
        PT = mem["f1_w"][:, 0:8 * SW].rearrange("p (h n) -> p h n", n=SW)
        Yq = mem["w2"][:, 4:8, :].rearrange("p (a b) d -> p a (b d)", a=2)
        yn = mem["w2"][:, 0:4, :].rearrange("p (a t) d -> p a t d", a=2)
        yT = mem["w2"][:, 8:10, :].rearrange("p b d -> p (b d)")
        rden = sb("rden", [P, 2, 4])
        res = mem["RES"]
        stats = sb("stats", [P, 2, 6])
        mv = sb("mv", [P, 2, 2, 2])
        var = sb("var", [P, 2])
        rstd = sb("rstd", [P, 2])
        neg_half = sb("neghalf", [P, 2])
        S = [ctx.enter_context(nc.psum_tensor(f"a1_S{i}", [P, 512], F32)) for i in range(2)]
        ST = [ctx.enter_context(nc.psum_tensor(f"a1_ST{i}", [P, 512], F32)) for i in range(2)]
        YP = ctx.enter_context(nc.psum_tensor("a1_YP", [P, 512], F32))
        PJ = ctx.enter_context(nc.psum_tensor("a1_PJ", [P, 512], F32))
        TR = ctx.enter_context(nc.psum_tensor("a1_TR", [P, 512], F32))
        MI = ctx.enter_context(nc.psum_tensor("a1_MI", [P, 512], F32))

        consts, ones_step = sem("consts"), sem("ones_step")
        stacked, fixed, zeroed = mem["stacked"], mem["fixed"], mem["zeroed"]
        pj_read = sem("pj_read")
        s_ready, max_done = sem("s_ready"), sem("max_done")
        mm_ready = sem("mm_ready")
        mxh_ready, mx_ready = sem("mxh_ready"), sem("mx_ready")
        mt_ready, mT_ready = sem("mt_ready"), sem("mT_ready")
        m_rows = sem("m_rows")
        st_ready, e_ready, p_ready = sem("st_ready"), sem("e_ready"), sem("p_ready")
        y_ready, yq_ready = sem("y_ready"), sem("yq_ready")
        yt_ready, den_ready, yn_ready = sem("yt_ready"), sem("den_ready"), sem("yn_ready")
        z_ready, yT_ready = sem("z_ready"), sem("yT_ready")
        o_ready = sem("o_ready")
        res_ready, ln_step, var_ready, rstd_ready, x_done = (sem(n) for n in "res_ready ln_step var_ready rstd_ready x_done".split())
        block, before, x_final = mem["block"], mem["before"], mem["x_done"]

        PREP = {0: "x", 4: "q", 8: "k", 17: "v"}
        PREP_AHEAD = AHEAD + 20
        EARLY = 2
        FIRST_V = -14
        MAX = 4
        AV, TQ, ZT, OUT = 3, 6, 15, 18
        HASTE = 7
        FIRST, LAST = -AHEAD, NH + OUT + 3 - HASTE

        NEXT = NH + 2

        ALONE = 4 * ((NH - AHEAD + 5) // 4)

        def st_bank(g):
            return (ST + S)[g % 4] if g >= ALONE else ST[g % 2]

        def prep_at(g, lag=0):
            for at, k in PREP.items():
                b, off = divmod(g + PREP_AHEAD - lag - at, H1)
                if off == 0 and EARLY * (k != "v") + (k == "v") <= b < NB:
                    return b, k
            if g - lag == FIRST_V:
                return 0, "v"
            return None, ""

        def scores_at(g):
            return g + AHEAD if 0 <= g + AHEAD < NH else None

        def maxima_at(g, lag=MAX):
            b, k = divmod(g + AHEAD - (H1 - 1) - lag, H1)
            return b if k == 0 and 0 <= b < NB else None

        def head_at(g):
            return g if 0 <= g < NH else None

        def quad_at(g, lag):
            q, k = divmod(g - 3 - lag, 4)
            return q if k == 0 and 0 <= q < NH // 4 else None

        def out_at(g, lag):
            if g == NH - 1 + lag - HASTE:
                return NB - 1
            b, k = divmod(g - (H1 - 1) - lag, H1)
            return b if k == 0 and 0 <= b < NB - 1 else None

        @block.sync
        def _(sp):
            sp.wait_ge(*before)
            prep_fixed(sp, mem, 1)
            prep_stack(sp, mem, 1, 0)
            prep_stack(sp, mem, 1, 1)
            for g in range(FIRST, LAST):
                if maxima_at(g) is not None:
                    b = maxima_at(g)
                    sp.wait_ge(mT_ready, b + 1)
                    sp.dma_start(q4[b % BUFS][4:P:32, :].bitcast(F32), mT[:, :].bitcast(F32)).then_inc(m_rows, 16)
                b, k = prep_at(g, 3)
                if k in ("q", "k"):
                    t = "qk".index(k)
                    if b >= BUFS:
                        sp.wait_ge(st_ready, (b - BUFS + 1) * H1)
                    elif t == 0:
                        prep_fixed(sp, mem, b)
                    prep_stack(sp, mem, b, t)

        @block.gpsimd
        def _(pool):
            pool.wait_ge(*before)
            def zero_buffer(n):
                pool.memset(q4[n][:, :].bitcast(F32), 0.0).then_inc(zeroed, 1)
                pool.memset(k4[n][:, :].bitcast(F32), 0.0).then_inc(zeroed, 1)

            zero_buffer(1)
            pool.memset(neg_half[:, :], -0.5)
            pool.memset(V1[:, :, :, :, :], 0.0).then_inc(ones_step, 1)
            pool.wait_ge(ones_step, 1)
            pool.memset(V1[:, :, :, :, 8:9], 1.0).then_inc(consts, 1)
            zero_buffer(2)
            for g in range(FIRST, LAST):
                if head_at(g) is not None:
                    pool.wait_ge(e_ready, g + 1)
                    v = PT[:, g % 8, :].rearrange("p (a c n) -> p a c n", a=3, c=1)[:, 0:3:2, 0, :]
                    pool.affine_select(out=v, in_=v, compare_op=ALU.is_ge, fill=0.0, base=0,
                                       pattern=[[0, 2], [1, P]], channel_multiplier=-1).then_inc(p_ready, 1)
                b, k = prep_at(g, 1)
                if k in ("q", "k"):
                    prep_sum(pool, mem, b, "qk".index(k))
                b, k = prep_at(g, 3)
                if k in ("q", "k"):
                    prep_low(pool, mem, b, "qk".index(k))
                if out_at(g, OUT + 2) is not None:
                    b = out_at(g, OUT + 2)
                    pool.wait_ge(var_ready, b + 1)
                    pool.tensor_tensor(rstd[:, :], var[:, :], neg_half[:, :], ALU.pow).then_inc(rstd_ready, 1)

        @block.scalar
        def _(act):
            act.wait_ge(*before)
            for g in range(FIRST, LAST):
                if g == -3:
                    act.wait_ge(zeroed, 6)
                    act.activation(q4[3][:, :], q4[2][:, :].bitcast(F32), ACT.Copy).then_inc(zeroed, 1)
                    act.activation(k4[3][:, :], k4[2][:, :].bitcast(F32), ACT.Copy).then_inc(zeroed, 1)
                b, k = prep_at(g, 1)
                if k == "x":
                    prep_x_high(act, mem, b, TR)
                if k == "v":
                    act.wait_ge(mem["v_ready"], b + 1)
                    act.wait_ge(consts, 1)
                    act.activation(V1[:, b % 4, :, :, 0:D1], PJ[:, 0:L].rearrange("p (t h d) -> p t h d", t=2, d=D1), ACT.Copy).then_inc(pj_read, 1)
                b, k = prep_at(g, 2)
                if k == "x":
                    prep_x_full(act, mem, b, TR)
                if k in ("q", "k"):
                    prep_high(act, mem, b, "qk".index(k))
                if g == NEXT + 1:
                    block_high(act, mem, 0, S[0])
                if g == NEXT + 2:
                    block_full(act, mem, 0, S[0])
                if maxima_at(g, MAX + 1) is not None:
                    b = maxima_at(g, MAX + 1)
                    act.wait_ge(mt_ready, b + 1)
                    if b >= 1:
                        act.wait_ge(m_rows, 16 * b)
                    act.activation(mT[:, :], TR[0:32, 0:L], ACT.Copy).then_inc(mT_ready, 1)
                if head_at(g) is not None:
                    act.wait_ge(st_ready, g + 1)
                    if g >= 8:
                        act.wait_ge(y_ready, (g - 8) // 4 + 1)
                    act.activation(PT[:, g % 8, :], st_bank(g)[:, 0:SW], ACT.Exp, scale=D1 ** -0.5).then_inc(e_ready, 1)
                if quad_at(g, AV + 1) is not None:
                    q = quad_at(g, AV + 1)
                    act.wait_ge(y_ready, q + 1)
                    if q >= 2:
                        act.wait_ge(yt_ready, q - 1)
                    act.activation(Yq[:, q % 2, :], YP[:, 0:L], ACT.Copy).then_inc(yq_ready, 1)
                if out_at(g, ZT + 1) is not None:
                    b = out_at(g, ZT + 1)
                    act.wait_ge(z_ready, b + 1)
                    act.activation(yT[:, :], TR[:, 0:L], ACT.Copy).then_inc(yT_ready, 1)

        @block.vector
        def _(dve):
            dve.wait_ge(*before)
            for g in range(FIRST, LAST):
                b, k = prep_at(g, 1)
                if k == "x":
                    prep_x_low(dve, mem, b, TR)
                if k in ("q", "k"):
                    prep_rotate(dve, mem, b, "qk".index(k), PJ)
                if g == NEXT + 1:
                    block_low(dve, mem, 0, S[0])
                h = scores_at(g)
                if h is not None:
                    b = h // H1
                    dve.wait_ge(s_ready, h + 1)
                    if b >= 2 and h % H1 == 0:
                        dve.wait_ge(mm_ready, 2 * (b - 1))
                    dve.tensor_reduce(m3[:, b % 2, h % H1, :], S[h % 2][:, 0:SW].rearrange("p (a n) -> p a n", a=3), AX.X, ALU.max).then_inc(max_done, 1)
                if maxima_at(g, MAX - 2) is not None:
                    b = maxima_at(g, MAX - 2)
                    dve.wait_ge(max_done, (b + 1) * H1)
                    dve.tensor_tensor(mm[:, 1, :], m3[:, b % 2, :, 0], m3[:, b % 2, :, 1], ALU.max).then_inc(mm_ready, 1)
                    dve.tensor_copy(mm[:, 0, :], m3[:, b % 2, :, 2]).then_inc(mm_ready, 1)
                    dve.wait_ge(mm_ready, 2 * b + 2)
                    if b >= 1:
                        dve.wait_ge(mt_ready, b)
                    by_pair = mm[:, :, :].rearrange("p t (j r) -> p t r j", r=2)
                    for t in range(2):
                        i = dve.tensor_copy(mx[:, t, :, 0, :], by_pair[:, t])
                    i.then_inc(mxh_ready, 1)
                    dve.wait_ge(mxh_ready, b + 1)
                    for t in range(2):
                        i = dve.tensor_tensor(mx[:, t, :, 1, :], by_pair[:, t], mx[:, t, :, 0, :].bitcast(F32), ALU.subtract)
                    i.then_inc(mx_ready, 1)
                q = quad_at(g, TQ + 1)
                if q is not None:
                    b, qq = divmod(q, 4)
                    dve.wait_ge(yt_ready, q + 1)
                    yt = MI[:, 0:L].rearrange("p (t i c) -> p t i c", t=2, i=4)
                    dve.reciprocal(rden[:, :, :], yt[:, :, :, D1]).then_inc(den_ready, 1)
                    dve.wait_ge(den_ready, q + 1)
                    if b >= 2 and qq == 0:
                        dve.wait_ge(z_ready, b - 1)
                    for t in range(2):
                        i = dve.tensor_tensor(yn[:, b % 2, t, qq * 32:qq * 32 + 32].rearrange("p (i d) -> p i d", i=4),
                                              yt[:, t, :, 0:D1], rden[:, t, :, None].to_broadcast([P, 4, D1]), ALU.mult)
                    i.then_inc(yn_ready, 1)
                b = out_at(g, OUT + 1)
                if b is not None:
                    dve.wait_ge(o_ready, b + 1)
                    dve.tensor_tensor(res[:, b % 2, :, :], PJ[:, 0:2 * D].rearrange("p (t d) -> p t d", t=2), X[:, 2 * b:2 * b + 2, :], ALU.add).then_inc(res_ready, 1)
                    dve.wait_ge(res_ready, b + 1)
                    norm_stats(dve, res[:, b % 2], stats, mv[:, b % 2], var, 2, ln_step, 2 * b, var_ready)
                b = out_at(g, OUT + 3)
                if b is not None:
                    dve.wait_ge(rstd_ready, b + 1)
                    norm_apply(dve, X[:, 2 * b:2 * b + 2, :], res[:, b % 2], mv[:, b % 2], rstd, 2).then_inc(x_done, 1)

        def use_order():
            tr, pj = [], []
            for g in range(FIRST, LAST):
                b, k = prep_at(g)
                if k == "x":
                    tr.append(("x", b))
                elif k:
                    pj.append((k, b))
                if maxima_at(g) is not None:
                    tr.append(("m", maxima_at(g)))
                if out_at(g, ZT) is not None:
                    tr.append(("z", out_at(g, ZT)))
                if out_at(g, OUT) is not None:
                    pj.append(("o", out_at(g, OUT)))
            return tr, pj

        TR_USES, PJ_USES = use_order()

        @block.tensor
        def _(pe):
            pe.wait_ge(*before)
            def bank_free(uses, use):
                at = uses.index(use)
                if at == 0:
                    return
                k, b = uses[at - 1]
                if k == "x":
                    pe.wait_ge(mem["xT_ready"], b + 1)
                elif k == "m":
                    pe.wait_ge(mT_ready, b + 1)
                elif k == "z":
                    pe.wait_ge(yT_ready, b + 1)
                elif k in "qk":
                    pe.wait_ge(mem["rb_ready"], 2 * b + "qk".index(k) + 1)
                elif k == "v":
                    pe.wait_ge(pj_read, b + 1)
                else:
                    pe.wait_ge(res_ready, b + 1)

            for g in range(FIRST, LAST):
                b, k = prep_at(g)
                if k == "x":
                    if b == EARLY:
                        pe.wait_ge(*x_final)
                    bank_free(TR_USES, ("x", b))
                    prep_transpose(pe, mem, b, TR)
                elif k == "v":
                    bank_free(PJ_USES, (k, b))
                    pe.wait_ge(mem["xT_ready"], b + 1)
                    for t in range(2):
                        i = pe.matmul(PJ[:, t * P:(t + 1) * P], xT[:, b % 2, t * P:(t + 1) * P], mem["a1_wv"][:, :], start=True, stop=True)
                    i.then_inc(mem["v_ready"], 1)
                elif k:
                    bank_free(PJ_USES, (k, b))
                    prep_project(pe, mem, b, "qk".index(k), PJ)
                if g == NEXT:
                    pe.wait_ge(e_ready, NH)
                    pe.wait_ge(x_done, 2)
                    block_transpose(pe, mem, 0, S[0])
                h = scores_at(g)
                if h is not None:
                    b, hh = divmod(h, H1)
                    j, par = divmod(hh, 2)
                    if hh == 0:
                        pe.wait_ge(stacked, stacked_by(b))
                        if b < BUFS:
                            pe.wait_ge(fixed[b], 32)
                    if h >= 2:
                        pe.wait_ge(max_done, h - 1)
                    rows = slice(64 * par, 64 * par + 64)
                    qq, kk = q4[b % BUFS][rows, j * L:(j + 1) * L], k4[b % BUFS][rows, j * L:(j + 1) * L]
                    pe.matmul(S[h % 2][:, 0:L], qq[:, P:L], kk[:, 0:L], start=True, stop=False, skip_group_check=True)
                    pe.matmul(S[h % 2][:, L:SW], qq[:, 0:P], kk[:, 0:P], start=False, stop=False, skip_group_check=True)
                    pe.matmul(S[h % 2][:, P:SW], mem["ident_b"][:, :], mem["mask_b"][:, :], start=False, stop=True, skip_group_check=True).then_inc(s_ready, 1)
                    if g < 4:
                        for _ in range(8 if g < 2 - AHEAD else 1):
                            pe.matmul(YP[:, 0:256], mem["ident_b"][:, :], mem["mask_b"][:, 0:256], start=True, stop=True)
                if maxima_at(g) is not None:
                    b = maxima_at(g)
                    bank_free(TR_USES, ("m", b))
                    pe.wait_ge(mx_ready, b + 1)
                    for t in range(2):
                        i = pe.transpose(TR[0:32, t * P:(t + 1) * P], mx[:, t, :, :, :].rearrange("p r c j -> p (r c j)").bitcast(F32), ident[:, :])
                    i.then_inc(mt_ready, 1)
                if head_at(g) is not None:
                    b, hh = divmod(g, H1)
                    j, par = divmod(hh, 2)
                    if hh == 0:
                        pe.wait_ge(m_rows, 16 * (b + 1))
                    if ALONE <= g < ALONE + 4:
                        pe.wait_ge(e_ready, g - 1)
                        pe.wait_ge(max_done, NH)
                    elif g >= 2:
                        pe.wait_ge(e_ready, g - 3 if g >= ALONE else g - 1)
                    rows = slice(64 * par, 64 * par + 64)
                    qq, kk = q4[b % BUFS][rows, j * L:(j + 1) * L], k4[b % BUFS][rows, j * L:(j + 1) * L]
                    pe.matmul(st_bank(g)[:, 0:L], kk[:, 0:P], qq[:, 0:L], start=True, stop=True)
                    pe.matmul(st_bank(g)[:, L:SW], kk[:, P:L], qq[:, P:L], start=True, stop=True).then_inc(st_ready, 1)
                q = quad_at(g, AV)
                if q is not None:
                    b = q // 4
                    pe.wait_ge(p_ready, 4 * q + 4)
                    pe.wait_ge(pj_read, b + 1)
                    if q >= 1:
                        pe.wait_ge(yq_ready, q)
                    for t in range(2):
                        for i4 in range(4):
                            hg = 4 * q + i4
                            cols = slice(0, L) if t == 0 else slice(L, SW)
                            i = pe.matmul(YP[32 * i4:32 * i4 + 32, t * P:L], V1[:, b % 4, t, hg % H1, :], PT[:, hg % 8, cols],
                                          start=(t == 0), stop=(t == 1), skip_group_check=True)
                    i.then_inc(y_ready, 1)
                q = quad_at(g, TQ)
                if q is not None:
                    pe.wait_ge(yq_ready, q + 1)
                    if q >= 1:
                        pe.wait_ge(yn_ready, q)
                    for t in range(2):
                        i = pe.transpose(MI[:, t * P:(t + 1) * P], Yq[:, q % 2, t * P:(t + 1) * P], ident[:, :])
                    i.then_inc(yt_ready, 1)
                b = out_at(g, ZT)
                if b is not None:
                    bank_free(TR_USES, ("z", b))
                    pe.wait_ge(yn_ready, 4 * (b + 1))
                    for t in range(2):
                        i = pe.transpose(TR[:, t * P:(t + 1) * P], yn[:, b % 2, t, :], ident[:, :])
                    i.then_inc(z_ready, 1)
                b = out_at(g, OUT)
                if b is not None:
                    bank_free(PJ_USES, ("o", b))
                    pe.wait_ge(yT_ready, b + 1)
                    for t in range(2):
                        i = pe.matmul(PJ[:, t * D:(t + 1) * D], yT[:, t * P:(t + 1) * P], mem["a1_wo"][:, :], start=True, stop=True)
                    i.then_inc(o_ready, 1)
        mem["x_done"], mem["before"] = (x_done, NB), (res_ready, NB)


def experts1(nc, mem, dr, out):
    X = mem["X"]
    NS = NBLK * NE1
    ctx = ExitStack()
    with ctx:
        sb = lambda n, s, d=F32: ctx.enter_context(nc.sbuf_tensor("f1_" + n, s, d))
        sem = lambda n: mem["scope"].enter_context(nc.semaphore("f1_" + n))
        w_h, w_l, w3 = mem["f1_w_h"], mem["f1_w_l"], mem["f1_w3"]
        xT, xh, xl = mem["bxT"], mem["bxh"], mem["bxl"]
        xh.append(sb("xh", [P, BT], F32R)[:, :])
        xl.append(sb("xl", [P, BT], F32R)[:, :])
        sc = sb("sc", [P, NT, NE1])
        top = sb("top", [P, NT, 8])
        idx = sb("idx", [P, NT, 8], U32)
        idf = sb("idf", [P, NT, 2])
        dlt = sb("dlt", [P, NT])
        ex = sb("ex", [P, NT])
        prob = sb("prob", [P, 2, NT])
        den = sb("den", [P, NT])
        oh = sb("oh", [P, 2, NT, NE1])
        gate = sb("gate", [P, NT, NE1])
        e_base = sb("e_base", [P, NT])
        sg = sb("sg", [P, 4, BT])
        hid = sb("hid", [P, 2, FC1, BT])
        acc = sb("acc", [P, 2, TB, D])
        fin = sb("fin", [P, 2, TB, D])
        stats = sb("stats", [P, TB, 6])
        mv = sb("mv", [P, 2, TB, 2])
        var = sb("var", [P, TB])
        rstd = sb("rstd", [P, TB])
        neg_half = sb("neghalf", [P, TB])
        T = ctx.enter_context(nc.psum_tensor("f1_T", [P, 512], F32))
        G = ctx.enter_context(nc.psum_tensor("f1_G", [P, 512], F32))
        H = [[ctx.enter_context(nc.psum_tensor(f"f1_H{i}{k}", [P, 512], F32)) for k in range(2)] for i in range(2)]
        O = [ctx.enter_context(nc.psum_tensor(f"f1_O{i}", [P, 512], F32)) for i in range(2)]
        g_ready, sc_ready, top_ready, idx_ready, g_step, gate_ready = (sem(n) for n in "g_ready sc_ready top_ready idx_ready g_step gate_ready".split())
        dlt_ready, ex_ready = sem("dlt_ready"), sem("ex_ready")
        h1_ready, h2_ready = sem("h1_ready"), sem("h2_ready")
        silu_done, hid_done = sem("silu_done"), sem("hid_done")
        o_ready, acc_done = sem("o_ready"), sem("acc_done")
        ln_step, var_ready, rstd_ready, fin_ready, consts = (sem(n) for n in "ln_step var_ready rstd_ready fin_ready consts".split())
        stored = [sem("stored0"), sem("stored1")]
        block, before, x_final = mem["block"], mem["before"], mem["x_done"]

        @block.sync
        def _(sp):
            sp.wait_ge(*before)
            for i in range(NBLK):
                sp.wait_ge(fin_ready, i + 1)
                sp.dma_start(out[:, TB * i:TB * i + TB, :], fin[:, i % 2, :, :]).then_inc(stored[i % 2], 16)
            for p in range(2):
                sp.wait_ge(stored[p], 16 * NBLK // 2)

        def exp_delta(pool, i):
            tt = slice(TB * i, TB * i + TB)
            pool.wait_ge(dlt_ready, i + 1)
            pool.tensor_tensor(ex[:, tt], e_base[:, tt], dlt[:, tt], ALU.pow).then_inc(ex_ready, 1)

        @block.gpsimd
        def _(pool):
            pool.wait_ge(*before)
            pool.memset(neg_half[:, :], -0.5).then_inc(consts, 1)
            pool.memset(e_base[:, :], float(np.e)).then_inc(consts, 1)
            pool.wait_ge(consts, 2)
            for i in range(NBLK):
                if i == 0:
                    exp_delta(pool, 0)
                if i + 1 < NBLK:
                    exp_delta(pool, i + 1)
                pool.wait_ge(var_ready, i + 1)
                pool.tensor_tensor(rstd[:, :], var[:, :], neg_half[:, :], ALU.pow).then_inc(rstd_ready, 1)

        def prepare_at(n, c, at):
            i, e = divmod(n, NE1)
            if c != FC1 - 1:
                return None
            if at >= 1 and n == at - 1:
                return 0
            return i + 1 if e == 4 + at and i + 1 < NBLK else None

        @block.scalar
        def _(act):
            act.wait_ge(*before)
            for n in range(NS):
                for c in range(FC1):
                    m = n * FC1 + c
                    act.wait_ge(h1_ready, m + 1)
                    if m >= 4:
                        act.wait_ge(hid_done, m - 3)
                    act.activation(sg[:, m % 4, :], H[m % 2][0][:, :], ACT.Silu).then_inc(silu_done, 1)
                    i = prepare_at(n, c, 0)
                    if i is not None:
                        if i >= 2:
                            act.wait_ge(h2_ready, (i - 1) * NE1 * FC1)
                        block_high(act, mem, i, T)
                        act.wait_ge(g_ready, i)
                        block_full(act, mem, i, T)

        @block.vector
        def _(dve):
            dve.wait_ge(*before)
            def top_two(i):
                tiles = range(TB * i, TB * i + TB)
                tt = slice(TB * i, TB * i + TB)
                dve.wait_ge(g_ready, i + 1)
                dve.tensor_copy(sc[:, tt, :], G[:, i * TB * NE1:(i + 1) * TB * NE1].rearrange("p (t e) -> p t e", e=NE1)).then_inc(sc_ready, 1)
                dve.wait_ge(sc_ready, i + 1)
                for t in tiles:
                    k = dve.max(top[:, t, :], sc[:, t, :])
                k.then_inc(top_ready, 1)
                dve.wait_ge(top_ready, i + 1)
                dve.tensor_tensor(dlt[:, tt], top[:, tt, 1], top[:, tt, 0], ALU.subtract).then_inc(dlt_ready, 1)
                for t in tiles:
                    k = dve.max_index(idx[:, t, :], top[:, t, :], sc[:, t, :])
                k.then_inc(idx_ready, 1)

            def gates(i):
                tt = slice(TB * i, TB * i + TB)

                def chain(ins, count):
                    ins.then_inc(g_step, 1)
                    dve.wait_ge(g_step, 8 * i + count)
                dve.wait_ge(idx_ready, i + 1)
                chain(dve.tensor_copy(idf[:, tt, :], idx[:, tt, 0:2]), 1)
                for k in range(2):
                    chain(dve.tensor_tensor(oh[:, k, tt, :], mem["iota8"][:, None, :].to_broadcast([P, TB, NE1]),
                                            idf[:, tt, k:k + 1].to_broadcast([P, TB, NE1]), ALU.is_equal), 2 + k)
                dve.wait_ge(ex_ready, i + 1)
                chain(dve.tensor_scalar(den[:, tt], ex[:, tt], 1.0, None, ALU.add), 4)
                chain(dve.reciprocal(prob[:, 0, tt], den[:, tt]), 5)
                chain(dve.tensor_tensor(prob[:, 1, tt], prob[:, 0, tt], ex[:, tt], ALU.mult), 6)
                for k in range(2):
                    chain(dve.tensor_tensor(oh[:, k, tt, :], oh[:, k, tt, :], prob[:, k, tt, None].to_broadcast([P, TB, NE1]), ALU.mult), 7 + k)
                dve.tensor_tensor(gate[:, tt, :], oh[:, 0, tt, :], oh[:, 1, tt, :], ALU.add).then_inc(gate_ready, 1)
                dve.wait_ge(gate_ready, i + 1)

            def combine(n):
                i, e = divmod(n, NE1)
                dve.wait_ge(o_ready, n + 1)
                if e > 0:
                    dve.wait_ge(acc_done, n)
                for t in range(TB):
                    prior = X[:, TB * i + t, :] if e == 0 else acc[:, i % 2, t, :]
                    k = dve.scalar_tensor_tensor(acc[:, i % 2, t, :], O[n % 2][:, t * D:(t + 1) * D], gate[:, TB * i + t, e:e + 1],
                                                 prior, ALU.mult, ALU.add)
                k.then_inc(acc_done, 1)

            def finish(i):
                dve.wait_ge(acc_done, (i + 1) * NE1)
                norm_stats(dve, acc[:, i % 2], stats, mv[:, i % 2], var, TB, ln_step, 2 * i, var_ready)

            def finish2(i):
                dve.wait_ge(rstd_ready, i + 1)
                if i >= 2:
                    dve.wait_ge(stored[i % 2], 16 * (i // 2))
                norm_apply(dve, fin[:, i % 2], acc[:, i % 2], mv[:, i % 2], rstd, TB).then_inc(fin_ready, 1)

            for n in range(NS + 2):
                for c in range(FC1):
                    m = n * FC1 + c
                    if n < NS:
                        dve.wait_ge(silu_done, m + 1)
                        dve.wait_ge(h2_ready, m + 1)
                        if n >= 2 and c == 0:
                            dve.wait_ge(o_ready, n - 1)
                        dve.tensor_tensor(hid[:, n % 2, c, :], H[m % 2][1][:, :], sg[:, m % 4, :], ALU.mult).then_inc(hid_done, 1)
                        if prepare_at(n, c, 0) is not None:
                            block_low(dve, mem, prepare_at(n, c, 0), T)
                if n >= 2:
                    combine(n - 2)
                    if (n - 2) % NE1 == NE1 - 1:
                        finish((n - 2) // NE1)
                if n >= 3 and (n - 3) % NE1 == NE1 - 1:
                    finish2((n - 3) // NE1)
                if prepare_at(n, FC1 - 1, 1) is not None:
                    top_two(prepare_at(n, FC1 - 1, 1))
                if prepare_at(n, FC1 - 1, 2) is not None:
                    gates(prepare_at(n, FC1 - 1, 2))
            finish2(NBLK - 1)

        @block.tensor
        def _(pe):
            pe.wait_ge(*before)
            def gate_scores(i):
                pe.wait_ge(mem["bxT_ready"], i + 1)
                if i >= 1:
                    pe.wait_ge(sc_ready, i)
                for t in range(TB):
                    col = (i * TB + t) * NE1
                    k = pe.matmul(G[:, col:col + NE1], xT[:, t * P:(t + 1) * P], mem["f1_wg"][:, :], start=True, stop=True)
                k.then_inc(g_ready, 1)

            for n in range(NS + 1):
                i, e = divmod(n, NE1)
                for c in range(FC1):
                    m = n * FC1 + c
                    if n < NS:
                        if e == 0 and c == 0:
                            pe.wait_ge(mem["bxl_ready"], i + 1)
                        if m >= 2:
                            pe.wait_ge(hid_done, m - 1)
                        for w, done in enumerate((h1_ready, h2_ready)):
                            col = (2 * e + w) * F1 + c * P
                            three_pass(pe, H[m % 2][w][:, :], w_h[:, col:col + P], w_l[:, col:col + P], xh[i % 2], xl[i % 2]).then_inc(done, 1)
                        if prepare_at(n, c, 0) is not None:
                            if prepare_at(n, c, 0) == NBLK - 1:
                                pe.wait_ge(*x_final)
                            pe.wait_ge(mem["bxT_ready"], prepare_at(n, c, 0))
                            block_transpose(pe, mem, prepare_at(n, c, 0), T)
                        if prepare_at(n, c, 1) is not None:
                            gate_scores(prepare_at(n, c, 1))
                    if n >= 1:
                        r = n - 1
                        if c == 0:
                            pe.wait_ge(hid_done, n * FC1)
                            if r >= 2:
                                pe.wait_ge(acc_done, r - 1)
                        for t in (2 * c, 2 * c + 1):
                            for f in range(FC1):
                                k = pe.matmul(O[r % 2][:, t * D:(t + 1) * D], hid[:, r % 2, f, t * P:(t + 1) * P],
                                              w3[:, (r % NE1) * FC1 + f, :], start=(f == 0), stop=(f == FC1 - 1))
                if n >= 1:
                    k.then_inc(o_ready, 1)


def program(nc, dr, out):
    ctx = ExitStack()
    with ctx, nc.Block() as block:
        sb = lambda n, s, d=F32: ctx.enter_context(nc.sbuf_tensor(n, s, d))
        sem = lambda n: ctx.enter_context(nc.semaphore(n))
        mem = dict(X=sb("X", [P, NT, D]), RES=sb("RES", [P, 2, 2, D]), ident=sb("ident", [P, P]),
                   w1=sb("w1", [P, NE0, HID]), w1_h=sb("w1_h", [P, NE0, HID], F32R), w1_l=sb("w1_l", [P, NE0, HID], F32R),
                   w2=sb("w2", [P, NE0 * HC, D]), b1=sb("b1", [P, NE0 * HC]), b2=sb("b2", [P, NE0, D]),
                   gate_w=sb("gate_w", [P, 2]), w_split=sem("w_split"), block=block, scope=ctx)
        mem["f0_xh"], mem["f0_xl"] = ([[sb(f"f0_x{name}00", [P, BT], F32R)[:, :], sb(f"f0_x{name}01", [P, BT], F32R)[:, :], None],
                                       [None] * NE0] for name in "hl")
        mem["f0_x0"] = mem["w1"][:, 0, :]
        mem["f0_sc"], mem["f0_pick0"] = sb("f0_sc", [P, TB, 2]), sb("f0_pick0", [P, TB])
        for name in "t_ready xh_ready xl_ready xT_ready gate_ready sc_ready pick_ready x0_ready".split():
            mem["f0_" + name] = sem("f0_" + name)
        in_w1, in_f0 = sem("in_w1"), sem("in_f0")
        mem["in_w1"], mem["in_f0"] = in_w1, in_f0

        def load_later(sp):
            dma_in(sp, mem["w1"][:, :, :], dr["f0_w1"], in_w1)
            for name in ("w2", "b1", "b2", "gate_w"):
                dma_in(sp, mem[name][(slice(None),) * len(mem[name].shape)], dr["f0_" + name], in_f0)
            dma_in(sp, mem["ident"][:, :], dr["ident"], in_f0)

        def wait_later(sp):
            sp.wait_ge(in_f0, 80)

        mem["load_later"], mem["wait_later"] = load_later, wait_later
        attention0(nc, mem, dr)
        ctx2 = ExitStack()
        with ctx2:
            sb = lambda n, s, d=F32: ctx2.enter_context(nc.sbuf_tensor(n, s, d))
            WC = 2 * NE1 * F1
            mem |= dict(f1_w=sb("f1_w", [P, WC]), f1_w_h=sb("f1_w_h", [P, WC], F32R), f1_w_l=sb("f1_w_l", [P, WC], F32R),
                        f1_w3=sb("f1_w3", [P, NE1 * FC1, D]), f1_wg=sb("f1_wg", [P, NE1]), iota8=sb("iota8", [P, NE1]),
                        a1_wqk=sb("a1_wqk", [P, 4 * P]), a1_wqk_h=sb("a1_wqk_h", [P, 4 * P], F32R), a1_wqk_l=sb("a1_wqk_l", [P, 4 * P], F32R),
                        a1_wv=sb("a1_wv", [P, P]), a1_wo=sb("a1_wo", [P, P]), rope=sb("rope", [P, 2, L]),
                        ident_b=sb("ident_b", [P, P], BF16), mask_b=sb("mask_b", [P, L], BF16))
            in_q, in_f1, in_l1 = sem("in_q"), sem("in_f1"), sem("in_l1")
            mem["xT"] = sb("a1_xT", [P, 2, L])
            for e, name in enumerate(("ra", "rb", "rq")):
                mem[name] = mem["w1"][:, e, :].rearrange("p (t n) -> p t n", t=2)
            for name in ("xh", "xl", "c_h", "c_l"):
                mem[name] = sb("a1_" + name, [P, 2, L], F32R)
            mem |= dict(q4=[sb("a1_q4_0", [P, NPAIR * L], F32R)], k4=[sb("a1_k4_0", [P, NPAIR * L], F32R)],
                        zero_rows=sb("a1_zero_rows", [32, L]), neg_rows=sb("a1_neg_rows", [32, L]))
            for name in "xt_ready xh_ready xl_ready xT_ready qk_ready v_ready ra_ready rb_ready rq_ready ch_ready cl_ready stacked zeroed".split():
                mem[name] = ctx.enter_context(nc.semaphore("a1_" + name))
            for name, of in (("bxh", "xh"), ("bxl", "xl"), ("bxT", "xT")):
                mem[name] = mem[of][:, :, :].rearrange("p a n -> p (a n)")
            mem["bxh"], mem["bxl"] = [mem["bxh"]], [mem["bxl"]]
            for name in "bt_ready bxh_ready bxl_ready bxT_ready".split():
                mem[name] = ctx.enter_context(nc.semaphore("f1_" + name))
            mem["fixed"] = [ctx.enter_context(nc.semaphore(f"a1_fixed{n}")) for n in range(BUFS)]

            names = ("f1_w3", "f1_wg", "iota8", "a1_wv", "a1_wo", "rope", "ident_b", "mask_b")
            mem["rope_loaded"] = (in_l1, 16 * len(names))

            def load_layer1(sp):
                dma_in(sp, mem["a1_wqk"][:, :], dr["a1_wqk"], in_q)
                dma_in(sp, mem["f1_w"][:, :], dr["f1_w"], in_f1)
                for name in names:
                    dma_in(sp, mem[name][(slice(None),) * len(mem[name].shape)], dr[name], in_l1)
                prep_fixed(sp, mem, 0)
                sp.wait_ge(in_l1, 16 * len(names))

            mem["load_layer1"] = load_layer1
            half = lambda n, k: mem[n][:, k * WC // 2:(k + 1) * WC // 2]
            mem["splits"] = [[], [(mem["a1_wqk"][:, :], mem["a1_wqk_h"][:, :], mem["a1_wqk_l"][:, :], in_q, 4 * P)]] + [
                [(half("f1_w", k), half("f1_w_h", k), half("f1_w_l", k), in_f1, WC // 2)] for k in range(2)]
            feed_forward0(nc, mem, dr)
            attention1(nc, mem, dr)
            experts1(nc, mem, dr, out)


def layouts(i):
    f = lambda a: np.ascontiguousarray(a)
    x = np.asarray(i["L0_attn_hidden_states"]).reshape(N, D)
    a = {"xT": f(x.T), "x": f(x.reshape(NT, P, D).transpose(1, 0, 2))}
    heads = [[2 * (2 * aa + g) + par for par in range(2) for _ in range(FD) for aa in range(4)] for g in range(2)]
    feats = [ff for _ in range(2) for ff in range(FD) for _ in range(4)]
    cols = [np.array(heads[g]) * FD + np.array(feats) for g in range(2)]
    a["a0_wqk"] = f(np.stack([np.asarray(i[w]).T[:, cols[g]] for w in ("L0_attn_Wq", "L0_attn_Wk") for g in range(2)], 1))
    a["a0_wv"] = f(np.asarray(i["L0_attn_Wv"]).T)
    a["a0_wo"] = f(np.asarray(i["L0_attn_Wo"]).T.reshape(NPAIR, P, D).transpose(1, 0, 2))
    a["a0_g"] = f(np.tile(np.asarray(i["L0_attn_g_weight"]), 2).reshape(P, 1))
    m, n = np.arange(P)[:, None], np.arange(P)[None, :]
    tri = (m <= n).astype(np.float32)
    a["mask0"] = f(np.concatenate([tri, np.ones((P, P), np.float32), tri], 1))
    ss, es = np.zeros((P, NPAIR, 32), np.float32), np.zeros((P, NPAIR, P), np.float32)
    for j in range(NPAIR):
        for par in range(2):
            for part in range(2):
                ss[64 * par:64 * par + 64, j, 4 * part + 2 * (j // 4) + par] = 1
                es[32 * (j % 4) + 4 * part + 2 * (j // 4) + par, j, 64 * par:64 * par + 64] = 1
    a["sum_sel"], a["exp_sel"] = ss, es
    a["low_row"] = f(np.where(np.arange(P) % 32 // 4 == 1, -1.0, 0.0).astype(np.float32).reshape(P, 1))
    a["ident"] = np.eye(P, dtype=np.float32)
    g = lambda n: np.asarray(i["L0_ffn_" + n])
    a["f0_w1"] = f(np.stack([g("w1")[0], g("sw1"), g("w1")[1]], 1))
    a["f0_w2"] = f(np.concatenate([g("w2")[0], g("sw2"), g("w2")[1]], 0).reshape(NE0 * HC, P, D).transpose(1, 0, 2))
    a["f0_b1"] = f(np.concatenate([g("b1")[0], g("sb1"), g("b1")[1]]).reshape(NE0 * HC, P).T)
    a["f0_b2"] = f(np.broadcast_to(np.stack([g("b2")[0], g("sb2"), g("b2")[1]])[None], (P, NE0, D)))
    a["f0_gate_w"] = f(g("gate_w").T)
    wqkv = np.asarray(i["L1_attn_W_qkv"])
    col = np.array([(2 * j + par) * D1 + d for par in range(2) for d in range(D1) for j in range(NPAIR)])
    swap = col // D1 * D1 + (col % D1 + D1 // 2) % D1
    a["a1_wqk"] = f(np.concatenate([wqkv[:, part * D + c] for part in range(2) for c in (col, swap)], 1))
    a["a1_wv"] = f(wqkv[:, 2 * D:])
    a["a1_wo"] = f(np.asarray(i["L1_attn_W_o"]))
    freqs = np.arange(D1 // 2, dtype=np.float32) / np.float32(D1 // 2)
    theta = np.float32(1.0) / np.float32(10000.0) ** freqs
    ang = np.arange(L, dtype=np.float32)[None, :] * theta[(col % D1) % (D1 // 2)][:, None]
    sign = np.where(col % D1 < D1 // 2, -1.0, 1.0).astype(np.float32)[:, None]
    a["rope"] = f(np.stack([np.cos(ang), sign * np.sin(ang)], 1).astype(np.float32))
    bf16 = mybir.dt.np(BF16)
    a["ident_b"] = np.eye(P).astype(bf16)
    a["mask_b"] = f(np.tile(np.where(n > m, -3e38, 0.0), (1, 2)).astype(bf16))
    h = lambda n: np.asarray(i["L1_ffn_" + n])
    a["f1_w"] = f(np.stack([h("W1"), h("W2")], 1).reshape(2 * NE1 * F1, D).T)
    a["f1_w3"] = f(h("W3").transpose(0, 2, 1).reshape(NE1 * FC1, P, D).transpose(1, 0, 2))
    a["f1_wg"] = f(h("Wg").T)
    a["iota8"] = f(np.broadcast_to(np.arange(NE1, dtype=np.float32), (P, NE1)))
    return a


def kernel(**inputs):
    import concourse.bacc as bacc
    from concourse.bass_utils import run_bass_kernel_spmd

    arrays = layouts(inputs)
    nc = bacc.Bacc("TRN2", target_bir_lowering=False, num_devices=1)
    dr = {n: nc.dram_tensor("in_" + n, a.shape, mybir.dt.from_np(a.dtype), kind="ExternalInput").ap() for n, a in arrays.items()}
    out = nc.dram_tensor("out", (N, D), F32, kind="ExternalOutput").ap()
    program(nc, dr, out.rearrange("(t p) d -> p t d", p=P))
    r = run_bass_kernel_spmd(nc, [{"in_" + n: a for n, a in arrays.items()}], core_ids=[0])
    return r.results[0]["out"].reshape(NB, L, D)
```
